# Optimizing a Trainium2 kernel written in Bass

```python
import numpy as np
import jax
import jax.numpy as jnp

def _softmax(x, axis=-1):
    return jax.nn.softmax(x, axis=axis)

def _gelu(x):
    return jax.nn.gelu(x, approximate=True)

def _silu(x):
    return jax.nn.silu(x)

def _sigmoid(x):
    return jax.nn.sigmoid(x)

def _layernorm(x, axis=-1, eps=1e-05):
    m = jnp.mean(x, axis=axis, keepdims=True)
    v = jnp.var(x, axis=axis, keepdims=True)
    return (x - m) / jnp.sqrt(v + eps)

def _scatter_add(tgt, idx, src, axis=0):
    return tgt.at[idx].add(src)

def _segment_sum(src, seg, n):
    return jax.ops.segment_sum(src, seg, n)
kernel_name = 'mk_gnn_resnorm_d2_gnn_r8_034087'

def setup_inputs(seed: int=0):
    np.random.seed(seed)
    _w = jnp.asarray

    def _rec_inputs():
        import jax
        import jax.numpy as jnp
        _gk = jax.random.key(seed)
        x = -0.0003713 + 1 * jax.random.normal(jax.random.fold_in(_gk, 1), (6250, 256), jnp.float32)
        src = jax.random.randint(jax.random.fold_in(_gk, 2), (200000,), 0, 6250, jnp.int32)
        dst = jax.random.randint(jax.random.fold_in(_gk, 3), (200000,), 0, 6250, jnp.int32)
        _o = jnp.argsort(dst, stable=True)
        src = src[_o]
        dst = dst[_o]
        edge_attr_16 = 0.000254156 + 0.999948 * jax.random.normal(jax.random.fold_in(_gk, 11), (200000, 16), jnp.float32)
        return (x, src, dst, edge_attr_16)
    x, src, dst, edge_attr_16 = _rec_inputs()

    def _L0_gnn_setup():
        import jax, jax.numpy as jnp
        import numpy as np
        N = 6250
        E = 100000
        F = 256
        H = 8
        C1 = 32
        C2 = 32
        ED = 16
        NEG_SLOPE = 0.2

        def gat_conv(x, src, dst, edge_attr, W, att_src, att_dst, W_e, att_e, bias, n_nodes):
            Hh, C = att_src.shape
            xp = (x @ W).reshape(-1, Hh, C)
            a_src = jnp.einsum('nhc,hc->nh', xp, att_src)
            a_dst = jnp.einsum('nhc,hc->nh', xp, att_dst)
            w_e = jnp.einsum('dhc,hc->dh', W_e.reshape(-1, Hh, C), att_e)
            a_edge = edge_attr @ w_e
            alpha = a_src[src] + a_dst[dst] + a_edge
            alpha = jax.nn.leaky_relu(alpha, NEG_SLOPE)
            m = jax.lax.stop_gradient(jax.ops.segment_max(alpha, dst, num_segments=n_nodes))
            ex = jnp.exp(alpha - m[dst])
            denom = jax.ops.segment_sum(ex, dst, num_segments=n_nodes)
            alpha = ex / (denom[dst] + 1e-16)
            msg = xp[src] * alpha[:, :, None]
            out = jax.ops.segment_sum(msg, dst, num_segments=n_nodes)
            return out.reshape(n_nodes, Hh * C) + bias
        key = jax.random.key(seed)
        ks = jax.random.split(key, 16)
        s = 0.05
        f32 = jnp.float32
        return {'x': jax.random.normal(ks[0], (N, F), f32), 'edge_index': jax.random.randint(ks[1], (2, E), 0, N, dtype=jnp.int32), 'edge_attr': jax.random.normal(ks[2], (E, ED), f32), 'W1': jax.random.normal(ks[3], (F, H * C1), f32) * s, 'att_src1': jax.random.normal(ks[4], (H, C1), f32) * s, 'att_dst1': jax.random.normal(ks[5], (H, C1), f32) * s, 'W_e1': jax.random.normal(ks[6], (ED, H * C1), f32) * s, 'att_e1': jax.random.normal(ks[7], (H, C1), f32) * s, 'b1': jnp.zeros((H * C1,), f32), 'W2': jax.random.normal(ks[8], (H * C1, H * C2), f32) * s, 'att_src2': jax.random.normal(ks[9], (H, C2), f32) * s, 'att_dst2': jax.random.normal(ks[10], (H, C2), f32) * s, 'W_e2': jax.random.normal(ks[11], (ED, H * C2), f32) * s, 'att_e2': jax.random.normal(ks[12], (H, C2), f32) * s, 'b2': jnp.zeros((H * C2,), f32)}
    _L0_gnn_all = _L0_gnn_setup()
    _L0_gnn_in = {k: v for k, v in _L0_gnn_all.items() if k in ('W1', 'att_src1', 'att_dst1', 'W_e1', 'att_e1', 'b1', 'W2', 'att_src2', 'att_dst2', 'W_e2', 'att_e2', 'b2')}
    del _L0_gnn_all

    def _L1_gnn_setup():
        import jax, jax.numpy as jnp
        import numpy as np
        N_NODES = 3125
        N_EDGES = 50000
        D_IN = 256
        D_OUT = 256
        HEADS = 8
        HEAD_DIM = D_OUT // HEADS
        NEG_SLOPE = 0.2
        LN_EPS = 1e-05

        def layer_norm(x, g, b):
            mu = jnp.mean(x, axis=-1, keepdims=True)
            var = jnp.mean((x - mu) ** 2, axis=-1, keepdims=True)
            return (x - mu) * jax.lax.rsqrt(var + LN_EPS) * g + b

        def gelu_tanh(x):
            c = np.sqrt(2.0 / np.pi).astype(np.float32)
            return 0.5 * x * (1.0 + jnp.tanh(c * (x + 0.044715 * x ** 3)))
        key = jax.random.key(seed)
        ks = jax.random.split(key, 16)
        s_in = 1.0 / np.sqrt(D_IN)
        s_out = 1.0 / np.sqrt(D_OUT)
        s_ff = 1.0 / np.sqrt(4 * D_OUT)
        return {'x': jax.random.normal(ks[0], (N_NODES, D_IN), jnp.float32), 'edge_index': jax.random.randint(ks[1], (2, N_EDGES), 0, N_NODES, jnp.int64), 'W': jax.random.normal(ks[2], (D_IN, HEADS * HEAD_DIM), jnp.float32) * s_in, 'att_src': jax.random.normal(ks[3], (HEADS, HEAD_DIM), jnp.float32) * s_out, 'att_dst': jax.random.normal(ks[4], (HEADS, HEAD_DIM), jnp.float32) * s_out, 'bias': jnp.zeros((D_OUT,), jnp.float32), 'W_res': jax.random.normal(ks[5], (D_IN, D_OUT), jnp.float32) * s_in, 'ln1_g': jnp.ones((D_IN,), jnp.float32), 'ln1_b': jnp.zeros((D_IN,), jnp.float32), 'ln2_g': jnp.ones((D_OUT,), jnp.float32), 'ln2_b': jnp.zeros((D_OUT,), jnp.float32), 'ffn_w1': jax.random.normal(ks[6], (D_OUT, 4 * D_OUT), jnp.float32) * s_out, 'ffn_b1': jnp.zeros((4 * D_OUT,), jnp.float32), 'ffn_w2': jax.random.normal(ks[7], (4 * D_OUT, D_OUT), jnp.float32) * s_ff, 'ffn_b2': jnp.zeros((D_OUT,), jnp.float32)}
    _L1_gnn_all = _L1_gnn_setup()
    _L1_gnn_in = {k: v for k, v in _L1_gnn_all.items() if k in ('W', 'att_src', 'att_dst', 'bias', 'W_res', 'ln1_g', 'ln1_b', 'ln2_g', 'ln2_b', 'ffn_w1', 'ffn_b1', 'ffn_w2', 'ffn_b2')}
    del _L1_gnn_all
    return {'x': x, 'src': src, 'dst': dst, 'edge_attr_16': edge_attr_16, 'L0_gnn_W1': _L0_gnn_in['W1'], 'L0_gnn_att_src1': _L0_gnn_in['att_src1'], 'L0_gnn_att_dst1': _L0_gnn_in['att_dst1'], 'L0_gnn_W_e1': _L0_gnn_in['W_e1'], 'L0_gnn_att_e1': _L0_gnn_in['att_e1'], 'L0_gnn_b1': _L0_gnn_in['b1'], 'L0_gnn_W2': _L0_gnn_in['W2'], 'L0_gnn_att_src2': _L0_gnn_in['att_src2'], 'L0_gnn_att_dst2': _L0_gnn_in['att_dst2'], 'L0_gnn_W_e2': _L0_gnn_in['W_e2'], 'L0_gnn_att_e2': _L0_gnn_in['att_e2'], 'L0_gnn_b2': _L0_gnn_in['b2'], 'L1_gnn_W': _L1_gnn_in['W'], 'L1_gnn_att_src': _L1_gnn_in['att_src'], 'L1_gnn_att_dst': _L1_gnn_in['att_dst'], 'L1_gnn_bias': _L1_gnn_in['bias'], 'L1_gnn_W_res': _L1_gnn_in['W_res'], 'L1_gnn_ln1_g': _L1_gnn_in['ln1_g'], 'L1_gnn_ln1_b': _L1_gnn_in['ln1_b'], 'L1_gnn_ln2_g': _L1_gnn_in['ln2_g'], 'L1_gnn_ln2_b': _L1_gnn_in['ln2_b'], 'L1_gnn_ffn_w1': _L1_gnn_in['ffn_w1'], 'L1_gnn_ffn_b1': _L1_gnn_in['ffn_b1'], 'L1_gnn_ffn_w2': _L1_gnn_in['ffn_w2'], 'L1_gnn_ffn_b2': _L1_gnn_in['ffn_b2']}

def reference(x, src, dst, edge_attr_16, L0_gnn_W1, L0_gnn_att_src1, L0_gnn_att_dst1, L0_gnn_W_e1, L0_gnn_att_e1, L0_gnn_b1, L0_gnn_W2, L0_gnn_att_src2, L0_gnn_att_dst2, L0_gnn_W_e2, L0_gnn_att_e2, L0_gnn_b2, L1_gnn_W, L1_gnn_att_src, L1_gnn_att_dst, L1_gnn_bias, L1_gnn_W_res, L1_gnn_ln1_g, L1_gnn_ln1_b, L1_gnn_ln2_g, L1_gnn_ln2_b, L1_gnn_ffn_w1, L1_gnn_ffn_b1, L1_gnn_ffn_w2, L1_gnn_ffn_b2):
    import jax
    import jax.numpy as jnp

    def _L0_gnn_ref(x, edge_index, edge_attr, W1, att_src1, att_dst1, W_e1, att_e1, b1, W2, att_src2, att_dst2, W_e2, att_e2, b2):
        import jax, jax.numpy as jnp
        import numpy as np
        N = 6250
        E = 100000
        F = 256
        H = 8
        C1 = 32
        C2 = 32
        ED = 16
        NEG_SLOPE = 0.2

        def gat_conv(x, src, dst, edge_attr, W, att_src, att_dst, W_e, att_e, bias, n_nodes):
            Hh, C = att_src.shape
            xp = (x @ W).reshape(-1, Hh, C)
            a_src = jnp.einsum('nhc,hc->nh', xp, att_src)
            a_dst = jnp.einsum('nhc,hc->nh', xp, att_dst)
            w_e = jnp.einsum('dhc,hc->dh', W_e.reshape(-1, Hh, C), att_e)
            a_edge = edge_attr @ w_e
            alpha = a_src[src] + a_dst[dst] + a_edge
            alpha = jax.nn.leaky_relu(alpha, NEG_SLOPE)
            m = jax.lax.stop_gradient(jax.ops.segment_max(alpha, dst, num_segments=n_nodes))
            ex = jnp.exp(alpha - m[dst])
            denom = jax.ops.segment_sum(ex, dst, num_segments=n_nodes)
            alpha = ex / (denom[dst] + 1e-16)
            msg = xp[src] * alpha[:, :, None]
            out = jax.ops.segment_sum(msg, dst, num_segments=n_nodes)
            return out.reshape(n_nodes, Hh * C) + bias
        src, dst = (edge_index[0], edge_index[1])
        h = jax.nn.relu(x)
        h = gat_conv(h, src, dst, edge_attr, W1, att_src1, att_dst1, W_e1, att_e1, b1, N)
        h = jax.nn.relu(h)
        h = gat_conv(h, src, dst, edge_attr, W2, att_src2, att_dst2, W_e2, att_e2, b2, N)
        return h + x

    def _L1_gnn_ref(x, edge_index, W, att_src, att_dst, bias, W_res, ln1_g, ln1_b, ln2_g, ln2_b, ffn_w1, ffn_b1, ffn_w2, ffn_b2):
        import jax, jax.numpy as jnp
        import numpy as np
        N_NODES = 3125
        N_EDGES = 50000
        D_IN = 256
        D_OUT = 256
        HEADS = 8
        HEAD_DIM = D_OUT // HEADS
        NEG_SLOPE = 0.2
        LN_EPS = 1e-05

        def layer_norm(x, g, b):
            mu = jnp.mean(x, axis=-1, keepdims=True)
            var = jnp.mean((x - mu) ** 2, axis=-1, keepdims=True)
            return (x - mu) * jax.lax.rsqrt(var + LN_EPS) * g + b

        def gelu_tanh(x):
            c = np.sqrt(2.0 / np.pi).astype(np.float32)
            return 0.5 * x * (1.0 + jnp.tanh(c * (x + 0.044715 * x ** 3)))
        N = x.shape[0]
        xn = layer_norm(x, ln1_g, ln1_b)
        loops = jnp.arange(N, dtype=edge_index.dtype)
        src = jnp.concatenate([edge_index[0], loops])
        dst = jnp.concatenate([edge_index[1], loops])
        h = (xn @ W).reshape(N, HEADS, HEAD_DIM)
        a_src = jnp.einsum('nhd,hd->nh', h, att_src)
        a_dst = jnp.einsum('nhd,hd->nh', h, att_dst)
        e = jax.nn.leaky_relu(a_src[src] + a_dst[dst], NEG_SLOPE)
        emax = jax.ops.segment_max(e, dst, num_segments=N)
        ee = jnp.exp(e - emax[dst])
        denom = jax.ops.segment_sum(ee, dst, num_segments=N)
        alpha = ee / denom[dst]
        msg = h[src] * alpha[:, :, None]
        agg = jax.ops.segment_sum(msg, dst, num_segments=N)
        out = agg.reshape(N, HEADS * HEAD_DIM) + xn @ W_res + bias
        out = layer_norm(out, ln2_g, ln2_b)
        ff = gelu_tanh(out @ ffn_w1 + ffn_b1) @ ffn_w2 + ffn_b2
        return out + ff
    edge_index = jnp.stack([src, dst])
    x = _layernorm(x + _L0_gnn_ref(x, edge_index, edge_attr_16, L0_gnn_W1, L0_gnn_att_src1, L0_gnn_att_dst1, L0_gnn_W_e1, L0_gnn_att_e1, L0_gnn_b1, L0_gnn_W2, L0_gnn_att_src2, L0_gnn_att_dst2, L0_gnn_W_e2, L0_gnn_att_e2, L0_gnn_b2), axis=-1)
    x = _layernorm(x + _L1_gnn_ref(x, edge_index, L1_gnn_W, L1_gnn_att_src, L1_gnn_att_dst, L1_gnn_bias, L1_gnn_W_res, L1_gnn_ln1_g, L1_gnn_ln1_b, L1_gnn_ln2_g, L1_gnn_ln2_b, L1_gnn_ffn_w1, L1_gnn_ffn_b1, L1_gnn_ffn_w2, L1_gnn_ffn_b2), axis=-1)
    return x

_drawn_inputs = setup_inputs


def setup_inputs(seed=0):
    import zlib

    import numpy as np

    out = dict(_drawn_inputs(seed))
    spreads = {'L0_gnn_b1': (0.0, 0.1),
     'L0_gnn_b2': (0.0, 0.1),
     'L1_gnn_bias': (0.0, 0.1),
     'L1_gnn_ln1_g': (1.0, 0.2),
     'L1_gnn_ln1_b': (0.0, 0.1),
     'L1_gnn_ln2_g': (1.0, 0.2),
     'L1_gnn_ln2_b': (0.0, 0.1),
     'L1_gnn_ffn_b1': (0.0, 0.1),
     'L1_gnn_ffn_b2': (0.0, 0.1)}
    factors = {'edge_attr_16': 8.0,
     'L0_gnn_att_src1': 28.14,
     'L0_gnn_att_dst1': 64.0,
     'L0_gnn_W_e1': 8.0,
     'L0_gnn_att_e1': 8.0,
     'L0_gnn_att_src2': 52.693,
     'L0_gnn_att_dst2': 64.0,
     'L0_gnn_W_e2': 8.0,
     'L0_gnn_att_e2': 8.0,
     'L1_gnn_att_dst': 3.601}
    for name, (base, spread) in spreads.items():
        noise = np.random.default_rng([zlib.crc32(name.encode()), seed]).standard_normal(out[name].shape)
        drawn = base * np.exp(spread * noise) if base else spread * noise
        out[name] = jnp.asarray(drawn.astype(out[name].dtype))
    for name, factor in factors.items():
        out[name] = (out[name] * factor).astype(out[name].dtype)
    return out
```

```python
import numpy as np
import concourse.bass as bass
from concourse import mybir
from contextlib import ExitStack

F32 = mybir.dt.float32
I32 = mybir.dt.int32
I16 = mybir.dt.int16
ALU = mybir.AluOpType
ACT = mybir.ActivationFunctionType
AX = mybir.AxisListType

N, E, F, H, C, ED = 6250, 200000, 256, 8, 32, 16
P = 128
HX = C + 1
ROW = H * HX
MSG = ROW + H + 1
WINDOWS = -(-N // P)
TILES = WINDOWS + WINDOWS % 2
NP = TILES * P
STEP = 512
J = STEP // P
S = 4
SLOTS = 3
STEPS = -(-(-(-E // STEP) + WINDOWS) // (S * SLOTS)) * (S * SLOTS)
MACROS = STEPS // S
ROUNDS = MACROS // SLOTS
EP = E + 2 * STEP
NO_NODE = 1 << 14
CP = 125
CC = E // CP
FF = 4 * F
FT = FF // P
KT = F // P
BIG = 1e30
VB1, VB2, VBIAS, VG1, VE1, VG2, VE2, VFB2 = range(8)


class Chain:

    def __init__(self, sem):
        self.sem, self.base, self.k, self.it, self.per = sem, 0, 0, None, 0

    def enter(self, it, first, per):
        self.base += self.k - first * per
        self.k, self.it, self.per = 0, it, per

    def leave(self, end):
        assert self.k == self.per, (self.k, self.per)
        self.base += end * self.per
        self.k, self.it, self.per = 0, None, 0

    def inc(self, ins):
        ins.then_inc(self.sem, 1)
        self.k += 1
        return self.k

    def wait(self, eng, k=None):
        k = self.k if k is None else k
        eng.wait_ge(self.sem, self.base + k if self.it is None else self.it * self.per + (self.base + k))


def build(nc, A, out):
    with ExitStack() as ctx:
        def sb(name, shape, dt=F32):
            return ctx.enter_context(nc.sbuf_tensor(name, shape, dt))

        def phase(run, *args):
            sems = []

            def sem(name):
                sems.append(nc.alloc_semaphore(name=name))
                return sems[-1]
            run(nc, sem, *args)
            nc.clear_and_free_semaphores(sems)
            nc.all_engine_barrier()

        htab = [nc.dram_tensor(f"htab{l}", [NP, ROW], F32).ap() for l in range(3)]
        x1_dram = nc.dram_tensor("x1_dram", [NP, F], F32).ap()
        res_dram = nc.dram_tensor("res_dram", [NP, F], F32).ap()

        m = {}
        m["acc"] = sb("acc", [P, TILES, H, HX])
        m["acc_max"] = sb("acc_max", [P, TILES, H])
        m["a_dst"] = sb("a_dst", [P, TILES, H])
        m["ident"] = sb("ident", [P, P])
        m["iota"] = sb("iota", [P, P])
        m["pidx"] = sb("pidx", [P, 1])
        m["last_row"] = sb("last_row", [P, S, J])
        m["w_base"] = sb("w_base", [P, STEPS])
        m["w_of"] = sb("w_of", [1, STEPS], I32)
        m["e_of"] = sb("e_of", [1, STEPS], I32)
        m["wx"] = [sb(f"wx{l}", [P, KT, ROW + H]) for l in range(3)]
        m["wres"] = sb("wres", [P, KT, F])
        m["webd"] = sb("webd", [S * ED, 2, S, H])
        m["vec"] = sb("vec", [P, 8, F])
        m["fb1"] = sb("fb1", [P, FT])
        m["gbuf"] = sb("gbuf", [P, SLOTS, S, J, MSG])
        m["onehot"] = sb("onehot", [P, SLOTS, S * J, P])
        m["onehot_t"] = sb("onehot_t", [P, S, STEP])
        m["dst_all"] = sb("dst_all", [P, S, STEP], I32)
        m["dst_h"] = sb("dst_h", [S * H, STEP], I32)
        m["ea"] = sb("ea", [S * ED, STEP])
        m["rec"] = sb("rec", [P, SLOTS, S, J, 4], I32)
        psum = ctx.enter_context(nc.psum_tensor("psum", [P, 8, 512], F32))

        phase(setup, A, m, psum)
        for l in range(3):
            phase(nodes_in, A, m, psum, l, htab, x1_dram, res_dram)
            phase(edges, A, m, psum, l, htab)
        phase(nodes_out, A, m, psum, x1_dram, res_dram, out)


def scratch(m, sizes):
    flat = m["gbuf"][:, :, :, :, :].rearrange("p a b c d -> p (a b c d)")
    at, got = 0, {}
    for name, shape in sizes.items():
        n = int(np.prod(shape))
        v = flat[:, at:at + n]
        if len(shape) == 2:
            v = v.rearrange("p (a b) -> p a b", a=shape[0])
        elif len(shape) == 3:
            v = v.rearrange("p (a b c) -> p a b c", a=shape[0], b=shape[1])
        got[name] = v
        at += n
    assert at <= SLOTS * S * J * MSG, at
    return got


def setup(nc, sem, A, m, psum):
    v = scratch(m, {"w_raw": (3, KT, F), "att": (8, F), "prod": (KT, F), "we_raw": (2, F),
                    "we": (2, H), "mask": (S, H), "ones": (P,), "thr": (1,), "istep": (STEPS,),
                    "cnt": (WINDOWS,), "diff": (WINDOWS,), "tri": (WINDOWS,), "size": (1,), "steps": (1,),
                    "coef": (1,), "coef_b": (P,), "first": (1,), "tmp": (1,)})
    reached = m["onehot"][:, 2, :, :].rearrange("p a b -> p (a b)")[:, 0:STEPS]
    dst_raw = m["onehot"][0:CP, 0, :, :].rearrange("p a b -> p (a b)").bitcast(I32)[:, 0:CC]
    dst_16 = m["onehot"][0:CP, 1, :, :].rearrange("p a b -> p (a b)").bitcast(I16)[:, 0:CC]
    junk_16 = m["onehot_t"][0:CP, :, :].rearrange("p a b -> p (a b)").bitcast(I16)[:, 0:CC]
    i_a = m["dst_h"][0:WINDOWS - 17, 0:1]
    del i_a
    ints = m["dst_all"][0:WINDOWS, 0, 0:2]
    dst_in, w_in, const, ps_done = sem("dst_in"), sem("w_in"), sem("const"), sem("setup_pe")
    dv, pool_own = sem("setup_dve"), sem("setup_pool")
    to_pe = sem("setup_to_pe")

    with nc.Block() as block:
        @block.sync
        def _(sp):
            sp.dma_start(dst_raw, A["dst"][0:E].rearrange("(p c) -> p c", p=CP)).then_inc(dst_in, 16)
            for l, w in enumerate(("L0_gnn_W1", "L0_gnn_W2", "L1_gnn_W")):
                sp.dma_start(v["w_raw"][:, l, :, :], A[w].rearrange("(k p) c -> p k c", p=P)).then_inc(w_in, 16)
            atts = ("L0_gnn_att_src1", "L0_gnn_att_dst1", "L0_gnn_att_src2", "L0_gnn_att_dst2",
                    "L1_gnn_att_src", "L1_gnn_att_dst", "L0_gnn_att_e1", "L0_gnn_att_e2")
            for i, a in enumerate(atts):
                sp.dma_start(v["att"][:, i, :], A[a].rearrange("h c -> (h c)").partition_broadcast(P)).then_inc(w_in, 16)
            for l, w in enumerate(("L0_gnn_W_e1", "L0_gnn_W_e2")):
                for s in range(S):
                    sp.dma_start(v["we_raw"][ED * s:ED * s + ED, l, :], A[w]).then_inc(w_in, 16)
            sp.dma_start(m["wres"][:, :, :], A["L1_gnn_W_res"].rearrange("(k p) c -> p k c", p=P)).then_inc(w_in, 16)
            vecs = ("L0_gnn_b1", "L0_gnn_b2", "L1_gnn_bias", "L1_gnn_ln1_g", "L1_gnn_ln1_b", "L1_gnn_ln2_g",
                    "L1_gnn_ln2_b", "L1_gnn_ffn_b2")
            for i, a in enumerate(vecs):
                sp.dma_start(m["vec"][:, i, :], A[a].partition_broadcast(P)).then_inc(w_in, 16)
            sp.dma_start(m["fb1"][:, :], A["ffn_b1_cols"]).then_inc(w_in, 16)
            sp.wait_ge(w_in, 16 * (3 + 8 + 2 * S + 1 + 8 + 1))
            sp.nop(nofuse=True)

        @block.gpsimd
        def _(pool):
            def own(ins, n=[0]):
                n[0] += 1
                ins.then_inc(pool_own, 1)
                pool.wait_ge(pool_own, n[0])
            own(pool.memset(m["ident"][:, :], 0.0))
            own(pool.affine_select(out=m["ident"][:, :], in_=m["ident"][:, :], compare_op=ALU.not_equal, fill=1.0,
                                   base=0, pattern=[[-1, P]], channel_multiplier=1))
            own(pool.iota(m["iota"][:, :], pattern=[[1, P]], base=0, channel_multiplier=0,
                          allow_small_or_imprecise_dtypes=True))
            own(pool.iota(m["pidx"][:, :], pattern=[[0, 1]], base=0, channel_multiplier=1,
                          allow_small_or_imprecise_dtypes=True))
            own(pool.iota(v["istep"], pattern=[[1, STEPS]], base=0, channel_multiplier=0,
                          allow_small_or_imprecise_dtypes=True))
            own(pool.memset(v["ones"], 1.0))
            own(pool.memset(v["tri"], 1.0))
            own(pool.affine_select(out=v["tri"], in_=v["tri"], compare_op=ALU.is_ge, fill=0.0,
                                   base=0, pattern=[[1, WINDOWS]], channel_multiplier=-1))
            own(pool.memset(m["last_row"][:, :, :], 0.0))
            own(pool.affine_select(out=m["last_row"][:, :, :], in_=m["last_row"][:, :, :], compare_op=ALU.not_equal,
                                   fill=1.0, base=-(J * P - 1), pattern=[[0, S], [1, J]], channel_multiplier=J))
            own(pool.memset(v["mask"], 1.0))
            own(pool.affine_select(out=v["mask"], in_=v["mask"], compare_op=ALU.is_ge, fill=0.0,
                                   base=0, pattern=[[-ED, S], [0, H]], channel_multiplier=1))
            own(pool.affine_select(out=v["mask"], in_=v["mask"], compare_op=ALU.is_ge, fill=0.0,
                                   base=ED - 1, pattern=[[ED, S], [0, H]], channel_multiplier=-1))
            pool.memset(m["acc_max"][:, :, :], -BIG).then_inc(const, 1)
            pool.memset(m["acc"][:, :, :, :], 0.0).then_inc(const, 1)

        @block.vector
        def _(dve):
            ch = Chain(dv)
            V = nc.vector
            cnt, diff = v["cnt"][0:CP, :], v["diff"][0:CP, :]
            dve.wait_ge(dst_in, 16)
            ch.inc(V.tensor_copy(dst_16, dst_raw))
            ch.inc(V.memset(cnt[:, 0:1], 0.0))
            ch.inc(V.memset(diff[:, 0:1], 0.0))
            ch.wait(dve)
            for w in range(1, WINDOWS):
                ch.inc(V.tensor_scalar(junk_16, dst_16, float(P * w), 0.0, ALU.is_lt, ALU.add,
                                       accum_out=cnt[:, w:w + 1]))
                ch.wait(dve)
            ch.inc(V.tensor_tensor(diff[:, 1:WINDOWS], cnt[:, 1:WINDOWS], cnt[:, 0:WINDOWS - 1], ALU.subtract))
            dve.wait_ge(const, 2)
            V.tensor_copy(v["tmp"], v["ones"][:, 0:1]).then_inc(to_pe, 1)
            dve.wait_ge(to_pe, 1)
            dve.wait_ge(ps_done, 1)
            size, steps = v["size"][0:WINDOWS, :], v["steps"][0:WINDOWS, :]
            ch.inc(V.tensor_copy(size, psum[0:WINDOWS, 0, 0:1]))
            ch.inc(V.tensor_scalar(ints[:, 0:1], psum[0:WINDOWS, 0, 0:1], float(STEP - 1), None, ALU.add))
            ch.wait(dve)
            ch.inc(V.tensor_scalar(ints[:, 1:2], ints[:, 0:1], STEP.bit_length() - 1, None, ALU.arith_shift_right))
            ch.wait(dve)
            ch.inc(V.tensor_copy(steps, ints[:, 1:2]))
            ch.wait(dve)
            ch.inc(V.scalar_tensor_tensor(v["coef"][0:WINDOWS, :], steps, -float(STEP), size, ALU.mult, ALU.add))
            ch.wait(dve)
            V.tensor_scalar(v["coef_b"][0:WINDOWS, :], v["ones"][0:WINDOWS, :], v["coef"][0:WINDOWS, 0:1], None,
                            ALU.mult).then_inc(to_pe, 1)
            dve.wait_ge(ps_done, 2)
            ch.inc(V.tensor_copy(v["first"][0:WINDOWS, :], psum[0:WINDOWS, 1, 0:1]))
            ch.wait(dve)
            V.tensor_scalar(reached[0:WINDOWS, :], v["istep"][0:WINDOWS, :], v["first"][0:WINDOWS, 0:1], None,
                            ALU.is_ge).then_inc(to_pe, 1)
            dve.wait_ge(ps_done, 3)
            ch.inc(V.tensor_scalar(m["w_base"][:, :], psum[:, 3, 0:STEPS], 1.0, float(P), ALU.subtract, ALU.mult))
            ch.inc(V.tensor_scalar(m["w_of"][:, :], psum[0:1, 3, 0:STEPS], 1.0, None, ALU.subtract))
            row = v["coef_b"][0:1, :]
            del row
            first_edge = m["onehot"][0:1, 2, 8:16, :].rearrange("p a b -> p (a b)")[:, 0:STEPS]
            ch.inc(V.scalar_tensor_tensor(first_edge, v["istep"][0:1, :], float(STEP), psum[0:1, 2, 0:STEPS],
                                          ALU.mult, ALU.add))
            ch.wait(dve)
            ch.inc(V.tensor_scalar(m["e_of"][:, :], first_edge, float(E), None, ALU.min))
            dve.wait_ge(w_in, 16 * (3 + 8 + 2 * S + 1 + 8 + 1))
            for l in range(3):
                for k in range(KT):
                    raw = v["w_raw"][:, l, k, :]
                    heads = m["wx"][l][:, k, 0:ROW].rearrange("p (h x) -> p h x", x=HX)
                    ch.inc(V.tensor_copy(heads[:, :, 0:C], raw.rearrange("p (h c) -> p h c", c=C)))
                    for d in range(2):
                        ch.inc(V.tensor_tensor(v["prod"][:, d, :], raw, v["att"][:, 2 * l + d, :], ALU.mult))
                        ch.wait(dve)
                        to = heads[:, :, C:HX].rearrange("p h o -> p (h o)") if d == 0 else m["wx"][l][:, k, ROW:ROW + H]
                        ch.inc(V.reduce_sum(to, v["prod"][:, d, :].rearrange("p (h c) -> p h c", c=C), axis=AX.X))
                        ch.wait(dve)
            K = S * ED
            for l in range(2):
                ch.inc(V.tensor_tensor(v["prod"][0:K, l, :], v["we_raw"][0:K, l, :], v["att"][0:K, 6 + l, :], ALU.mult))
                ch.wait(dve)
                ch.inc(V.reduce_sum(v["we"][0:K, l, :], v["prod"][0:K, l, :].rearrange("p (h c) -> p h c", c=C),
                                    axis=AX.X))
                ch.wait(dve)
                ch.inc(V.tensor_tensor(m["webd"][:, l, :, :], v["mask"][0:K, :, :],
                                       v["we"][0:K, l, :].unsqueeze(1).to_broadcast([K, S, H]), ALU.mult))

        @block.tensor
        def _(pe):
            T = nc.tensor
            pe.wait_ge(to_pe, 1)
            T.matmul(psum[0:WINDOWS, 0, 0:1], v["diff"][0:CP, :], v["ones"][0:CP, 0:1]).then_inc(ps_done, 1)
            pe.wait_ge(to_pe, 2)
            T.matmul(psum[0:WINDOWS, 1, 0:1], v["tri"][0:WINDOWS, :], v["steps"][0:WINDOWS, :]).then_inc(ps_done, 1)
            pe.wait_ge(to_pe, 3)
            T.matmul(psum[:, 2, 0:STEPS], v["coef_b"][0:WINDOWS, :], reached[0:WINDOWS, :])
            T.matmul(psum[:, 3, 0:STEPS], v["ones"][0:WINDOWS, :], reached[0:WINDOWS, :]).then_inc(ps_done, 1)


def load_tile(dram, t):
    return dram[bass.ds(t * P, P), :]


def nodes_in(nc, sem, A, m, psum, l, htab, x1_dram, res_dram):
    v = scratch(m, {"x_in": (2, F), "h_in": (2, F), "h_t": (2, KT, P), "row": (2, ROW), "den": (2, H),
                    "y": (2, F), "stat": (2, 6), "mv": (2, 2), "rstd": (2, 1), "mv2": (2, 2), "rstd2": (2, 1),
                    "xn": (2, F), "res": (2, F), "self": (2, H), "zeros": (ROW,), "eps": (1,)})
    zeros = v["zeros"].rearrange("p (h x) -> p h x", x=HX)
    n = f"_n{l}"
    x_in = [sem(f"x_in{i}" + n) for i in range(2)]
    row_out = [sem(f"row_out{i}" + n) for i in range(2)]
    x1_out = [sem(f"x1_out{i}" + n) for i in range(2)]
    res_out = [sem(f"res_out{i}" + n) for i in range(2)]
    act_ready, h_tr, h_t_ready, proj, row_ready, adst_done, own = (
        sem(k + n) for k in ("act_ready", "h_tr", "h_t_ready", "proj", "row_ready", "proj_used", "dve"))
    x1_ready, var_ready, std_ready, res_ready, pre_ready = (
        sem(k + n) for k in ("x1_ready", "var_ready", "std_ready", "res_ready", "pre_ready"))
    per_dve = {0: 2, 1: 12, 2: 58}[l]

    def pairs(eng, body, chain=None, per=0):
        for b in range(2):
            body(0, b)
        if chain:
            chain.enter(None, 0, 0)
        with eng.Fori(1, TILES // 2) as i:
            if chain:
                chain.enter(i, 1, per)
            for b in range(2):
                body(i, b)
            if chain:
                chain.leave(TILES // 2)

    with nc.Block() as block:
        @block.sync
        def _(sp):
            def body(i, b):
                t = i * 2 + b
                if l != 1:
                    if not isinstance(i, int):
                        sp.wait_ge(act_ready, t - 1)
                        sp.nop(nofuse=True)
                    sp.dma_start(v["x_in"][:, b, :], load_tile(A["x"], t)).then_inc(x_in[b], 16)
                if l == 2:
                    sp.wait_ge(x1_ready, t + 1)
                    sp.nop(nofuse=True)
                    sp.dma_start(load_tile(x1_dram, t), v["y"][:, b, :]).then_inc(x1_out[b], 16)
                    sp.wait_ge(res_ready, t + 1)
                    sp.nop(nofuse=True)
                    sp.dma_start(load_tile(res_dram, t), v["res"][:, b, :]).then_inc(res_out[b], 16)
                if l != 0:
                    sp.wait_ge(row_ready, t + 1)
                    sp.nop(nofuse=True)
                    sp.dma_start(load_tile(htab[l], t), v["row"][:, b, :]).then_inc(row_out[b], 16)
            pairs(sp, body)
            for b in range(2):
                if l == 2:
                    sp.wait_ge(x1_out[b], 16 * (TILES // 2))
                    sp.wait_ge(res_out[b], 16 * (TILES // 2))
                    sp.nop(nofuse=True)
                if l != 0:
                    sp.wait_ge(row_out[b], 16 * (TILES // 2))
                    sp.nop(nofuse=True)

        @block.gpsimd
        def _(pool):
            if l != 0:
                return

            def body(i, b):
                t = i * 2 + b
                pool.wait_ge(row_ready, t + 1)
                pool.nop(nofuse=True)
                pool.dma_start(load_tile(htab[l], t), v["row"][:, b, :]).then_inc(row_out[b], 16)
            pairs(pool, body)
            for b in range(2):
                pool.wait_ge(row_out[b], 16 * (TILES // 2))

        @block.scalar
        def _(act):
            def body(i, b):
                t = i * 2 + b
                if l == 0:
                    act.wait_ge(x_in[b], i * 16 + 16)
                    if not isinstance(i, int):
                        act.wait_ge(h_tr, t - 1)
                    nc.scalar.activation(v["h_in"][:, b, :], v["x_in"][:, b, :], ACT.Relu).then_inc(act_ready, 1)
                elif l == 1:
                    act.wait_ge(pre_ready, t + 1)
                    if not isinstance(i, int):
                        act.wait_ge(h_tr, t - 1)
                    nc.scalar.activation(v["h_in"][:, b, :], v["y"][:, b, :], ACT.Relu).then_inc(act_ready, 1)
                else:
                    for q in range(2):
                        act.wait_ge(var_ready, t * 2 + (q + 1))
                        mv, rs = (v["mv"], v["rstd"]) if q == 0 else (v["mv2"], v["rstd2"])
                        nc.scalar.activation(rs[:, b, :], mv[:, b, 1:2], ACT.Sqrt,
                                             bias=v["eps"][:, 0:1]).then_inc(std_ready, 1)
                act.wait_ge(h_tr, t + 1)
                if not isinstance(i, int):
                    act.wait_ge(proj, t - 1)
                nc.scalar.activation(v["h_t"][:, b, :, :], psum[:, b, 0:F].rearrange("p (k n) -> p k n", k=KT),
                                     ACT.Copy).then_inc(h_t_ready, 1)
                act.wait_ge(proj, t + 1)
                if not isinstance(i, int):
                    act.wait_ge(row_out[b], i * 16)
                nc.scalar.activation(v["row"][:, b, :], psum[:, 2 + b, 0:ROW], ACT.Copy).then_inc(row_ready, 1)
            act.wait_ge(own, 1)
            pairs(act, body)

        @block.tensor
        def _(pe):
            def body(i, b):
                t = i * 2 + b
                pe.wait_ge(act_ready, t + 1)
                if not isinstance(i, int):
                    pe.wait_ge(h_t_ready, t - 1)
                for k in range(KT):
                    last = nc.tensor.transpose(psum[:, b, k * P:(k + 1) * P], v["h_in"][:, b, k * P:(k + 1) * P],
                                               m["ident"][:, :])
                last.then_inc(h_tr, 1)
                pe.wait_ge(h_t_ready, t + 1)
                if not isinstance(i, int):
                    pe.wait_ge(row_ready, t - 1)
                    pe.wait_ge(adst_done, t - 1)
                for k in range(KT):
                    last = nc.tensor.matmul(psum[:, 2 + b, 0:ROW + H], v["h_t"][:, b, k, :], m["wx"][l][:, k, :],
                                            start=k == 0, stop=k == KT - 1)
                if l == 2:
                    for k in range(KT):
                        last = nc.tensor.matmul(psum[:, 4 + b, 0:F], v["h_t"][:, b, k, :], m["wres"][:, k, :],
                                                start=k == 0, stop=k == KT - 1)
                last.then_inc(proj, 1)
            pairs(pe, body)

        @block.vector
        def _(dve):
            ch = Chain(own)
            V = nc.vector

            def bc(ap, n):
                return ap.unsqueeze(2).to_broadcast([P, ap.shape[1], n])

            def normalised(i, b, t):
                acc = m["acc"][:, bass.ds(t, 1), :, :].rearrange("p o h x -> p (o h) x")
                den, y = v["den"][:, b, :], v["y"][:, b, :].rearrange("p (h c) -> p h c", c=C)
                ch.inc(V.tensor_scalar(den, acc[:, :, C:HX].rearrange("p h o -> p (h o)"), 1e-16, None, ALU.add))
                ch.wait(dve)
                ch.inc(V.reciprocal(den, den))
                ch.wait(dve)
                if l == 1 and not isinstance(i, int):
                    dve.wait_ge(act_ready, t - 1)
                if l == 2 and not isinstance(i, int):
                    dve.wait_ge(x1_out[b], i * 16)
                ch.inc(V.tensor_tensor(y, acc[:, :, 0:C], bc(den, C), ALU.mult))
                ch.wait(dve)
                return acc

            def stats(src, b, mv, rs, t, q):
                ch.inc(V.bn_stats(v["stat"][:, b, :], src))
                ch.wait(dve)
                dve.nop(nofuse=True)
                V.bn_aggr(v[mv][:, b, :], v["stat"][:, b, :]).then_inc(var_ready, 1)
                dve.wait_ge(std_ready, t * 2 + (q + 1))
                ch.inc(V.reciprocal(v[rs][:, b, :], v[rs][:, b, :]))
                ch.wait(dve)

            def body(i, b):
                t = i * 2 + b
                if l == 1:
                    acc = normalised(i, b, t)
                    V.tensor_tensor(v["y"][:, b, :], v["y"][:, b, :], m["vec"][:, VB1, :],
                                    ALU.add).then_inc(pre_ready, 1)
                    ch.inc(V.tensor_copy(acc, zeros))
                    ch.inc(V.tensor_scalar(m["acc_max"][:, bass.ds(t, 1), :].rearrange("p o h -> p (o h)"),
                                           zeros[:, :, 0], -BIG, None, ALU.add))
                if l == 2:
                    acc = normalised(i, b, t)
                    y = v["y"][:, b, :]
                    ch.inc(V.tensor_tensor(y, y, m["vec"][:, VB2, :], ALU.add))
                    ch.wait(dve)
                    dve.wait_ge(x_in[b], i * 16 + 16)
                    ch.inc(V.tensor_tensor(y, y, v["x_in"][:, b, :], ALU.add))
                    ch.wait(dve)
                    ch.inc(V.tensor_tensor(y, y, v["x_in"][:, b, :], ALU.add))
                    ch.wait(dve)
                    stats(y, b, "mv", "rstd", t, 0)
                    ch.inc(V.tensor_scalar(y, y, v["mv"][:, b, 0:1], v["rstd"][:, b, 0:1], ALU.subtract, ALU.mult))
                    ch.wait(dve)
                    dve.sem_inc(x1_ready, 1)
                    stats(y, b, "mv2", "rstd2", t, 1)
                    xn = v["xn"][:, b, :]
                    ch.inc(V.tensor_scalar(xn, y, v["mv2"][:, b, 0:1], v["rstd2"][:, b, 0:1],
                                           ALU.subtract, ALU.mult))
                    ch.wait(dve)
                    ch.inc(V.tensor_tensor(xn, xn, m["vec"][:, VG1, :], ALU.mult))
                    ch.wait(dve)
                    if not isinstance(i, int):
                        dve.wait_ge(h_tr, t - 1)
                    V.tensor_tensor(v["h_in"][:, b, :], xn, m["vec"][:, VE1, :], ALU.add).then_inc(act_ready, 1)
                dve.wait_ge(proj, t + 1)
                dve.wait_ge(row_ready, t + 1)
                logits = psum[:, 2 + b, 0:ROW].rearrange("p (h x) -> p h x", x=HX)
                to = m["a_dst"][:, bass.ds(t, 1), :].rearrange("p o h -> p (o h)")
                ch.inc(V.tensor_copy(to, psum[:, 2 + b, ROW:ROW + H]))
                if l == 2:
                    ch.inc(V.tensor_copy(acc, logits))
                    ch.wait(dve)
                    ch.inc(V.tensor_scalar(acc[:, :, C:HX].rearrange("p h o -> p (h o)"), zeros[:, :, 0], 1.0, None,
                                           ALU.add))
                    e = v["self"][:, b, :]
                    ch.inc(V.tensor_tensor(e, logits[:, :, C:HX].rearrange("p h o -> p (h o)"), to, ALU.add))
                    ch.wait(dve)
                    ch.inc(V.scalar_tensor_tensor(m["acc_max"][:, bass.ds(t, 1), :].rearrange("p o h -> p (o h)"),
                                                  e, 0.2, e, ALU.mult, ALU.max))
                    if not isinstance(i, int):
                        dve.wait_ge(res_out[b], i * 16)
                    ch.inc(V.tensor_tensor(v["res"][:, b, :], psum[:, 4 + b, 0:F], m["vec"][:, VBIAS, :], ALU.add))
                    ch.wait(dve)
                    dve.sem_inc(res_ready, 1)
                ch.wait(dve)
                dve.sem_inc(adst_done, 1)

            ch.inc(V.memset(v["eps"], 1e-5))
            ch.inc(V.memset(v["zeros"], 0.0))
            ch.wait(dve)
            k0 = ch.k
            body(0, 0)
            body(0, 1)
            per = ch.k - k0
            with dve.Fori(1, TILES // 2) as i:
                ch.enter(i, 1, per)
                body(i, 0)
                body(i, 1)
                ch.leave(TILES // 2)
            ch.wait(dve)


def edges(nc, sem, A, m, psum, l, htab):
    n = f"_e{l}"
    has_ea = l < 2
    rec_in = [sem(f"rec_in{k}" + n) for k in range(SLOTS)]
    gathered = [sem(f"gathered{k}" + n) for k in range(SLOTS)]
    dst_all_in, dst_h_in, ea_in = (sem(k + n) for k in ("dst_all_in", "dst_h_in", "ea_in"))
    (onehot_t_ready, onehot_ready, pre_ready, alpha_ready, alpha_t, alpha_t_sb, max_ready, max_back,
     max_used, diff_ready, exp_ready, weighted, summed, merged, rescale_ready, rescaled, own, masks_ready) = (
        sem(k + n) for k in ("onehot_t_ready", "onehot_ready", "pre_ready", "alpha_ready", "alpha_t", "alpha_t_sb",
                             "max_ready", "max_back", "max_used", "diff_ready", "exp_ready", "weighted", "summed",
                             "merged", "rescale_ready", "rescaled", "dve", "masks_ready"))
    gbuf, rec, onehot, onehot_t = m["gbuf"], m["rec"], m["onehot"], m["onehot_t"]
    psA = psum[:, 0, 0:J * S * H]
    psT = psum[0:S * H, 1, :]
    psR = psum[:, 2, 0:J * S * H]
    psM = psum[:, 4:8, :]

    with ExitStack() as ctx:
        def sb(name, shape, dt=F32):
            return ctx.enter_context(nc.sbuf_tensor(name + n, shape, dt))
        w4 = sb("w4", [P, SLOTS, S])
        nid4 = sb("nid4", [P, SLOTS, S])
        dl = sb("dl", [P, S, J])
        flag = sb("flag", [P, SLOTS, S, J])
        alpha = sb("alpha", [P, J, S * H])
        asum = sb("asum", [P, J, S * H])
        dif = sb("dif", [P, J, S * H])
        aT = sb("aT", [S * H, STEP])
        fwd = sb("fwd", [S * H, STEP])
        mx = sb("mx", [S * H, STEP])
        link = sb("link", [S * H, STEP + 1])
        part_max = sb("part_max", [P, S, H])
        untouched = sb("untouched", [P, S])
        old_max = sb("old_max", [P, S, H])
        new_max = sb("new_max", [P, S, H])
        d12 = sb("d12", [P, 2, S, H])
        r12 = sb("r12", [P, 2, S, H])
        part = sb("part", [P, 2, H, HX])

        def rounds(eng, body, chain=None, tail=None):
            for k in range(SLOTS):
                body(0, k)
            k0 = chain.k if chain else 0
            per = body.per if chain else 0
            with eng.Fori(1, ROUNDS - 1) as i:
                if chain:
                    chain.enter(i, 1, per)
                for k in range(SLOTS):
                    body(i, k)
                if chain:
                    chain.leave(ROUNDS - 1)
            for k in range(SLOTS):
                body(ROUNDS - 1, k)

        def has(i, k, d):
            return not isinstance(i, int) or 0 <= SLOTS * i + k + d < MACROS

        with nc.Block() as block:
            @block.sync
            def _(sp):
                def body(i, k):
                    M = i * SLOTS + k
                    at = [sp.value_load(m["e_of"][0:1, bass.ds(M * S + s, 1)], min_val=0, max_val=E) for s in range(S)]
                    if has(i, k, -SLOTS):
                        sp.wait_ge(gathered[k], i * (16 * S * J))
                        sp.nop(nofuse=True)
                        sp.wait_ge(onehot_ready, M - (SLOTS - 1))
                        sp.nop(nofuse=True)
                    for s in range(S):
                        sp.dma_start(rec[:, k, s, :, :].rearrange("p j f -> p (j f)"),
                                     A["records"][bass.ds(at[s], STEP), :].rearrange("(p j) f -> p (j f)", j=J)
                                     ).then_inc(rec_in[k], 16)
                    if has_ea:
                        if has(i, k, -1):
                            sp.wait_ge(pre_ready, M)
                            sp.nop(nofuse=True)
                        for s in range(S):
                            sp.dma_start(m["ea"][ED * s:ED * s + ED, :], A["ea_t"][:, bass.ds(at[s], STEP)]
                                         ).then_inc(ea_in, 16)
                    if has(i, k, -1):
                        sp.wait_ge(onehot_t_ready, M)
                        sp.nop(nofuse=True)
                    for s in range(S):
                        sp.dma_start(m["dst_all"][:, s, :], A["dst"][bass.ds(at[s], STEP)].partition_broadcast(P)
                                     ).then_inc(dst_all_in, 16)
                    if has(i, k, -1):
                        sp.wait_ge(masks_ready, M)
                        sp.nop(nofuse=True)
                    for s in range(S):
                        sp.dma_start(m["dst_h"][H * s:H * s + H, :], A["dst"][bass.ds(at[s], STEP)].partition_broadcast(H)
                                     ).then_inc(dst_h_in, 16)
                rounds(sp, body)

            @block.gpsimd
            def _(pool):
                def body(i, k):
                    M = i * SLOTS + k
                    pool.wait_ge(rec_in[k], i * (16 * S) + 16 * S)
                    if has(i, k, -SLOTS):
                        pool.wait_ge(summed, (M - (SLOTS - 1)) * S)
                    pool.nop(nofuse=True)
                    for s in range(S):
                        for j in range(J):
                            pool.indirect_dma_start(
                                out=gbuf[:, k, s, j, 0:ROW], out_offset=None, in_=htab[l],
                                in_offset=bass.IndirectOffsetOnAxis(ap=rec[:, k, s, j, 0:1], axis=0),
                            ).then_inc(gathered[k], 16)
                rounds(pool, body)

            @block.scalar
            def _(act):
                def rescale(M):
                    act.wait_ge(rescale_ready, M + 1)
                    nc.scalar.activation(r12[:, :, :, :].rearrange("p a s h -> p (a s h)"),
                                         d12[:, :, :, :].rearrange("p a s h -> p (a s h)"),
                                         ACT.Exp).then_inc(rescaled, 1)

                def body(i, k):
                    M = i * SLOTS + k
                    act.wait_ge(alpha_t, M + 1)
                    if has(i, k, -1):
                        act.wait_ge(max_ready, M)
                    nc.scalar.activation(aT[:, :], psT.rearrange("r (j p) -> r p j", j=J), ACT.Copy
                                         ).then_inc(alpha_t_sb, 1)
                    if has(i, k, -2):
                        rescale(M - 2)
                    act.wait_ge(diff_ready, M + 1)
                    ex = gbuf[:, k, :, :, 0:ROW].rearrange("p s j (h x) -> p j s h x", x=HX)[:, :, :, :, C]
                    for j in range(J):
                        last = nc.scalar.activation(ex[:, j, :, :],
                                                    dif[:, j, :].rearrange("p (s h) -> p s h", s=S), ACT.Exp)
                    last.then_inc(exp_ready, 1)
                rounds(act, body)
                for M in (MACROS - 2, MACROS - 1):
                    rescale(M)

            @block.tensor
            def _(pe):
                T = nc.tensor

                def logits(M):
                    pe.wait_ge(onehot_t_ready, M + 1)
                    if has_ea:
                        pe.wait_ge(ea_in, M * (16 * S) + 16 * S)
                    w = [pe.value_load(m["w_of"][0:1, bass.ds(M * S + s, 1)], min_val=0, max_val=WINDOWS - 1)
                         for s in range(S)]
                    for j in range(J):
                        if has_ea:
                            T.matmul(psA[:, j * S * H:(j + 1) * S * H], m["ea"][:, j:STEP:J],
                                     m["webd"][:, l, :, :].rearrange("p s h -> p (s h)"), start=True, stop=False)
                        for s in range(S):
                            c = (j * S + s) * H
                            last = T.matmul(psA[:, c:c + H], onehot_t[:, s, j:STEP:J],
                                            m["a_dst"][:, bass.ds(w[s], 1), :].rearrange("p o h -> p (o h)"),
                                            start=not has_ea, stop=not has_ea or s == S - 1)
                    last.then_inc(pre_ready, 1)

                def sums(i, k, M):
                    for s in range(S):
                        pe.wait_ge(weighted, M * S + (s + 1))
                        if has(i, k, -1):
                            pe.wait_ge(merged, M * S + (s + 1 - S))
                        for j in range(J):
                            last = T.matmul(psM[:, s, 0:MSG], onehot[:, k, s * J + j, :], gbuf[:, k, s, j, :],
                                            start=j == 0, stop=j == J - 1)
                        last.then_inc(summed, 1)

                def body(i, k):
                    M = i * SLOTS + k
                    pe.wait_ge(alpha_ready, M + 1)
                    if has(i, k, -1):
                        pe.wait_ge(alpha_t_sb, M)
                    for j in range(J):
                        last = T.transpose(psT[:, j * P:(j + 1) * P], alpha[:, j, :], m["ident"][:, :])
                    last.then_inc(alpha_t, 1)
                    if has(i, k, 1):
                        logits(M + 1)
                    pe.wait_ge(max_ready, M + 1)
                    if has(i, k, -1):
                        pe.wait_ge(max_used, M)
                    pe.nop(nofuse=True)
                    for j in range(J):
                        last = T.transpose(psR[:, j * S * H:(j + 1) * S * H], mx[:, j:STEP:J],
                                           m["ident"][0:S * H, 0:S * H])
                    last.then_inc(max_back, 1)
                    if has(i, k, -1):
                        if k > 0:
                            sums(i, k - 1, M - 1)
                        else:
                            sums(i if not isinstance(i, int) else i - 1, SLOTS - 1, M - 1)
                logits(0)
                rounds(pe, body)
                sums(ROUNDS - 1, SLOTS - 1, MACROS - 1)

            @block.vector
            def _(dve):
                ch = Chain(own)
                V = nc.vector
                st = {}

                def transposed_onehot(M, k):
                    dve.wait_ge(dst_all_in, M * (16 * S) + 16 * S)
                    ch.inc(V.tensor_copy(w4[:, k, :], m["w_base"][:, bass.ds(M * S, S)]))
                    ch.inc(V.tensor_scalar(nid4[:, k, :], m["w_base"][:, bass.ds(M * S, S)], m["pidx"][:, 0:1],
                                           None, ALU.add))
                    ch.wait(dve)
                    if not isinstance(M, int) or M > 0:
                        dve.wait_ge(pre_ready, M)
                    for s in range(S):
                        last = V.tensor_scalar(onehot_t[:, s, :], m["dst_all"][:, s, :], nid4[:, k, s:s + 1], None,
                                               ALU.is_equal)
                    last.then_inc(onehot_t_ready, 1)

                def edge_onehot(i, k, M):
                    dve.wait_ge(rec_in[k], i * (16 * S) + 16 * S)
                    r = rec[:, k, :, :, :]
                    ch.inc(V.tensor_tensor(dl[:, :, :], r[:, :, :, 1],
                                           w4[:, k, :].unsqueeze(2).to_broadcast([P, S, J]), ALU.subtract))
                    ch.inc(V.tensor_tensor(flag[:, k, :, :], r[:, :, :, 1], r[:, :, :, 2], ALU.not_equal))
                    ch.wait(dve)
                    ch.inc(V.tensor_tensor(flag[:, k, :, :], flag[:, k, :, :], m["last_row"][:, :, :], ALU.max))
                    V.tensor_tensor(onehot[:, k, :, :], m["iota"][:, :].unsqueeze(1).to_broadcast([P, S * J, P]),
                                    dl[:, :, :].rearrange("p s j -> p (s j)").unsqueeze(2).to_broadcast([P, S * J, P]),
                                    ALU.is_equal).then_inc(onehot_ready, 1)

                def merge_maxima(M):
                    dve.wait_ge(summed, M * S + S)
                    w = [dve.value_load(m["w_of"][0:1, bass.ds(M * S + s, 1)], min_val=0, max_val=WINDOWS - 1)
                         for s in range(S)]
                    st["w"] = w
                    ch.inc(V.tensor_scalar(untouched[:, :], psM[:, :, MSG - 1], 1.0, BIG, ALU.subtract, ALU.mult))
                    ch.wait(dve)
                    ch.inc(V.tensor_tensor(part_max[:, :, :], psM[:, :, ROW:ROW + H],
                                           untouched[:, :].unsqueeze(2).to_broadcast([P, S, H]), ALU.add))
                    ch.wait(dve)
                    for s in range(S):
                        am = m["acc_max"][:, bass.ds(w[s], 1), :].rearrange("p o h -> p (o h)")
                        ch.inc(V.tensor_copy(old_max[:, s, :], am))
                        ch.wait(dve)
                        ch.inc(V.tensor_tensor(am, old_max[:, s, :], part_max[:, s, :], ALU.max))
                        ch.wait(dve)
                    ch.inc(V.tensor_tensor(new_max[:, :, :], old_max[:, :, :], part_max[:, :, :], ALU.max))
                    ch.wait(dve)
                    ch.inc(V.tensor_tensor(d12[:, 0, :, :], old_max[:, :, :], new_max[:, :, :], ALU.subtract))
                    V.tensor_tensor(d12[:, 1, :, :], part_max[:, :, :], new_max[:, :, :],
                                    ALU.subtract).then_inc(rescale_ready, 1)

                def merge_sums(M):
                    w = st["w"]
                    dve.wait_ge(rescaled, M + 1)

                    def r(a, s):
                        return r12[:, a, s, :].unsqueeze(2).to_broadcast([P, H, HX])
                    adds = []
                    for s in range(S):
                        acc = m["acc"][:, bass.ds(w[s], 1), :, :].rearrange("p o h x -> p (o h) x")
                        V.tensor_tensor(part[:, s % 2, :, :], psM[:, s, 0:ROW].rearrange("p (h x) -> p h x", x=HX),
                                        r(1, s), ALU.mult).then_inc(merged, 1)
                        dve.wait_ge(merged, M * S + (s + 1))
                        ch.inc(V.tensor_tensor(acc, acc, r(0, s), ALU.mult))
                        ch.wait(dve)
                        ch.inc(V.tensor_tensor(acc, acc, part[:, s % 2, :, :], ALU.add))
                        ch.wait(dve)

                def body(i, k):
                    M = i * SLOTS + k
                    dve.wait_ge(pre_ready, M + 1)
                    dve.wait_ge(gathered[k], i * (16 * S * J) + 16 * S * J)
                    a_src = gbuf[:, k, :, :, 0:ROW].rearrange("p s j (h x) -> p j s h x", x=HX)[:, :, :, :, C]
                    ch.inc(V.tensor_tensor(asum[:, :, :].rearrange("p j (s h) -> p j s h", s=S),
                                           psA.rearrange("p (j s h) -> p j s h", j=J, s=S), a_src, ALU.add))
                    ch.wait(dve)
                    V.scalar_tensor_tensor(alpha[:, :, :], asum[:, :, :], 0.2, asum[:, :, :], ALU.mult,
                                           ALU.max).then_inc(alpha_ready, 1)
                    dve.wait_ge(dst_h_in, M * (16 * S) + 16 * S)
                    V.tensor_tensor(link[:, 1:STEP], m["dst_h"][:, 1:STEP], m["dst_h"][:, 0:STEP - 1],
                                    ALU.is_equal).then_inc(masks_ready, 1)
                    dve.wait_ge(masks_ready, M + 1)
                    ch.inc(V.tensor_scalar(link[:, 1:STEP], link[:, 1:STEP], 1.0, BIG, ALU.subtract, ALU.mult))
                    if has(i, k, -2):
                        merge_maxima(M - 2)
                    ch.wait(dve)
                    dve.wait_ge(alpha_t_sb, M + 1)
                    ch.inc(V.tensor_tensor_scan(fwd[:, :], link[:, 0:STEP], aT[:, :], -BIG, ALU.add, ALU.max))
                    ch.wait(dve)
                    V.tensor_tensor_scan(mx[:, ::-1], link[:, :0:-1], fwd[:, ::-1], -BIG,
                                         ALU.add, ALU.max).then_inc(max_ready, 1)
                    if has(i, k, -2):
                        merge_sums(M - 2)
                    dve.wait_ge(alpha_ready, M + 1)
                    dve.wait_ge(max_back, M + 1)
                    V.tensor_tensor(dif[:, :, :], alpha[:, :, :], psR.rearrange("p (j c) -> p j c", j=J),
                                    ALU.subtract).then_inc(diff_ready, 1)
                    dve.wait_ge(onehot_ready, M + 1)
                    V.tensor_tensor(gbuf[:, k, :, :, ROW:ROW + H].rearrange("p s j h -> p j s h"),
                                    psR.rearrange("p (j s h) -> p j s h", j=J, s=S),
                                    flag[:, k, :, :].rearrange("p s j -> p j s").unsqueeze(3)
                                    .to_broadcast([P, J, S, H]), ALU.mult).then_inc(max_used, 1)
                    ch.inc(V.tensor_copy(gbuf[:, k, :, :, MSG - 1], flag[:, k, :, :]))
                    if has(i, k, 1):
                        edge_onehot(*((i, k + 1) if k + 1 < SLOTS else (i + 1, 0)), M + 1)
                    dve.wait_ge(exp_ready, M + 1)
                    for s in range(S):
                        g = gbuf[:, k, s, :, 0:ROW].rearrange("p j (h x) -> p j h x", x=HX)
                        V.tensor_tensor(g[:, :, :, 0:C], g[:, :, :, 0:C],
                                        g[:, :, :, C:HX].to_broadcast([P, J, H, C]), ALU.mult).then_inc(weighted, 1)
                    if has(i, k, 2):
                        transposed_onehot(M + 2, (k + 2) % SLOTS)

                per = SLOTS * (1 + 1 + (2 + 2 * S + 2) + 1 + 2 * S + 1 + 3 + 2)
                body.per = per
                ch.inc(V.memset(link[:, :], -BIG))
                transposed_onehot(0, 0)
                transposed_onehot(1, 1)
                edge_onehot(0, 0, 0)
                rounds(dve, body, ch)
                for M in (MACROS - 2, MACROS - 1):
                    merge_maxima(M)
                    merge_sums(M)


def nodes_out(nc, sem, A, m, psum, x1_dram, res_dram, out):
    v = scratch(m, {"res": (2, F), "x1": (2, F), "o": (2, F), "o_t": (KT, 2 * P), "den": (2, H),
                    "stat": (2, 6), "mv": (2, 2), "rstd": (2, 1), "stat2": (2, 6), "mv2": (2, 2), "rstd2": (2, 1),
                    "y": (2, F), "eps": (1,), "w1": (KT, FF), "w2": (FT, F), "g": (FT, 2 * P)})
    w_in, own = sem("ffn_in"), sem("dve_o")
    in_ = [sem(f"node_in{i}") for i in range(2)]
    stored = [sem(f"stored{i}") for i in range(2)]
    (o_ready, o_tr, o_t_ready, up, gelu, down, var, std, var2, std2, out_ready) = (
        sem(k + "_o") for k in ("o_ready", "o_tr", "o_t_ready", "up", "gelu", "down", "var", "std", "var2", "std2",
                                "out_ready"))
    PAIRS = TILES // 2

    with nc.Block() as block:
        def pairs(eng, body):
            body(0)
            with eng.Fori(1, PAIRS) as i:
                body(i)

        @block.sync
        def _(sp):
            sp.dma_start(v["w1"], A["L1_gnn_ffn_w1"].rearrange("(k p) c -> p k c", p=P)).then_inc(w_in, 16)
            sp.dma_start(v["w2"], A["L1_gnn_ffn_w2"].rearrange("(k p) c -> p k c", p=P)).then_inc(w_in, 16)

            def body(i):
                for b in range(2):
                    if not isinstance(i, int):
                        sp.wait_ge(out_ready, i * 2 + (b - 1))
                        sp.nop(nofuse=True)
                    sp.dma_start(v["res"][:, b, :], load_tile(res_dram, i * 2 + b)).then_inc(in_[b], 16)
                    sp.dma_start(v["x1"][:, b, :], load_tile(x1_dram, i * 2 + b)).then_inc(in_[b], 16)
            pairs(sp, body)

        @block.gpsimd
        def _(pool):
            def body(i):
                for b in range(2):
                    pool.wait_ge(out_ready, i * 2 + (b + 1))
                    pool.nop(nofuse=True)
                    pool.dma_start(load_tile(out, i * 2 + b), v["y"][:, b, :]).then_inc(stored[b], 16)
            pairs(pool, body)
            for b in range(2):
                pool.wait_ge(stored[b], 16 * PAIRS)

        @block.scalar
        def _(act):
            act.wait_ge(own, 1)

            def body(i):
                for b in range(2):
                    act.wait_ge(var, i * 2 + (b + 1))
                    nc.scalar.activation(v["rstd"][:, b, :], v["mv"][:, b, 1:2], ACT.Sqrt,
                                         bias=v["eps"][:, 0:1]).then_inc(std, 1)
                act.wait_ge(o_tr, i + 1)
                if not isinstance(i, int):
                    act.wait_ge(up, i * FT)
                nc.scalar.activation(v["o_t"], psum[:, 0, :].rearrange("p (k n) -> p k n", k=KT),
                                     ACT.Copy).then_inc(o_t_ready, 1)
                for f in range(FT):
                    act.wait_ge(up, i * FT + (f + 1))
                    if not isinstance(i, int):
                        act.wait_ge(down, i * 2)
                    nc.scalar.activation(v["g"][:, f, :], psum[:, 1 + f % 3, 0:2 * P], ACT.Gelu_apprx_tanh,
                                         bias=m["fb1"][:, f:f + 1]).then_inc(gelu, 1)
                for b in range(2):
                    act.wait_ge(var2, i * 2 + (b + 1))
                    nc.scalar.activation(v["rstd2"][:, b, :], v["mv2"][:, b, 1:2], ACT.Sqrt,
                                         bias=v["eps"][:, 0:1]).then_inc(std2, 1)
            pairs(act, body)

        @block.tensor
        def _(pe):
            T = nc.tensor
            pe.wait_ge(w_in, 32)

            def body(i):
                pe.wait_ge(o_ready, i * 2 + 2)
                if not isinstance(i, int):
                    pe.wait_ge(o_t_ready, i)
                for b in range(2):
                    for k in range(KT):
                        last = T.transpose(psum[:, 0, (2 * k + b) * P:(2 * k + b + 1) * P],
                                           v["o"][:, b, k * P:(k + 1) * P], m["ident"][:, :])
                last.then_inc(o_tr, 1)
                pe.wait_ge(o_t_ready, i + 1)
                for f in range(FT):
                    if f >= 3 or not isinstance(i, int):
                        pe.wait_ge(gelu, i * FT + (f - 2))
                    for k in range(KT):
                        last = T.matmul(psum[:, 1 + f % 3, 0:2 * P], v["w1"][:, k, f * P:(f + 1) * P],
                                        v["o_t"][:, k, :], start=k == 0, stop=k == KT - 1)
                    last.then_inc(up, 1)
                for b in range(2):
                    if not isinstance(i, int):
                        pe.wait_ge(out_ready, i * 2 + (b - 1))
                    for f in range(FT):
                        if b == 0:
                            pe.wait_ge(gelu, i * FT + (f + 1))
                        last = T.matmul(psum[:, 4 + b, 0:F], v["g"][:, f, b * P:(b + 1) * P], v["w2"][:, f, :],
                                        start=f == 0, stop=f == FT - 1)
                    last.then_inc(down, 1)
            pairs(pe, body)

        @block.vector
        def _(dve):
            ch = Chain(own)
            V = nc.vector
            ch.inc(V.memset(v["eps"], 1e-5))
            ch.wait(dve)

            def body(i):
                for b in range(2):
                    t = i * 2 + b
                    acc = m["acc"][:, bass.ds(t, 1), :, :].rearrange("p o h x -> p (o h) x")
                    den, o = v["den"][:, b, :], v["o"][:, b, :]
                    ch.inc(V.reciprocal(den, acc[:, :, C:HX].rearrange("p h o -> p (h o)")))
                    ch.wait(dve)
                    ch.inc(V.tensor_tensor(o.rearrange("p (h c) -> p h c", c=C), acc[:, :, 0:C],
                                           den.unsqueeze(2).to_broadcast([P, H, C]), ALU.mult))
                    ch.wait(dve)
                    dve.wait_ge(in_[b], i * 32 + 32)
                    ch.inc(V.tensor_tensor(o, o, v["res"][:, b, :], ALU.add))
                    ch.wait(dve)
                    ch.inc(V.bn_stats(v["stat"][:, b, :], o))
                    ch.wait(dve)
                    dve.nop(nofuse=True)
                    V.bn_aggr(v["mv"][:, b, :], v["stat"][:, b, :]).then_inc(var, 1)
                    dve.wait_ge(std, t + 1)
                    ch.inc(V.reciprocal(v["rstd"][:, b, :], v["rstd"][:, b, :]))
                    ch.wait(dve)
                    ch.inc(V.tensor_scalar(o, o, v["mv"][:, b, 0:1], v["rstd"][:, b, 0:1], ALU.subtract, ALU.mult))
                    ch.wait(dve)
                    ch.inc(V.tensor_tensor(o, o, m["vec"][:, VG2, :], ALU.mult))
                    ch.wait(dve)
                    V.tensor_tensor(o, o, m["vec"][:, VE2, :], ALU.add).then_inc(o_ready, 1)
                for b in range(2):
                    t = i * 2 + b
                    y = v["y"][:, b, :]
                    dve.wait_ge(o_ready, t + 1)
                    if not isinstance(i, int):
                        dve.wait_ge(stored[b], i * 16)
                    ch.inc(V.tensor_tensor(y, v["o"][:, b, :], v["x1"][:, b, :], ALU.add))
                    ch.wait(dve)
                    ch.inc(V.tensor_tensor(y, y, m["vec"][:, VFB2, :], ALU.add))
                    ch.wait(dve)
                    dve.wait_ge(down, t + 1)
                    ch.inc(V.tensor_tensor(y, y, psum[:, 4 + b, 0:F], ALU.add))
                    ch.wait(dve)
                    ch.inc(V.bn_stats(v["stat2"][:, b, :], y))
                    ch.wait(dve)
                    dve.nop(nofuse=True)
                    V.bn_aggr(v["mv2"][:, b, :], v["stat2"][:, b, :]).then_inc(var2, 1)
                    dve.wait_ge(std2, t + 1)
                    ch.inc(V.reciprocal(v["rstd2"][:, b, :], v["rstd2"][:, b, :]))
                    ch.wait(dve)
                    V.tensor_scalar(y, y, v["mv2"][:, b, 0:1], v["rstd2"][:, b, 0:1], ALU.subtract,
                                    ALU.mult).then_inc(out_ready, 1)
            k0 = ch.k
            body(0)
            per = ch.k - k0
            with dve.Fori(1, PAIRS) as i:
                ch.enter(i, 1, per)
                body(i)
                ch.leave(PAIRS)


def kernel(**inputs):
    import concourse.bacc as bacc
    from concourse.bass_utils import run_bass_kernel_spmd

    a = {k: np.ascontiguousarray(v) for k, v in inputs.items()}
    x = np.pad(a["x"], ((0, NP - N), (0, 0)))
    src = np.pad(a["src"], (0, EP - E))
    dst = np.pad(a["dst"], (0, EP - E), constant_values=NO_NODE)
    arrays = {
        "x": x, "dst": dst,
        "records": np.ascontiguousarray(np.stack([src, dst, np.roll(dst, -1), np.zeros_like(dst)], axis=1)),
        "ea_t": np.ascontiguousarray(np.pad(a["edge_attr_16"], ((0, EP - E), (0, 0))).T),
        "ffn_b1_cols": np.ascontiguousarray(a["L1_gnn_ffn_b1"].reshape(FT, P).T),
    }
    for k in a:
        if k not in ("x", "src", "dst", "edge_attr_16", "L1_gnn_ffn_b1"):
            arrays[k] = a[k]
    nc = bacc.Bacc("TRN2", target_bir_lowering=False, num_devices=1)
    A = {k: nc.dram_tensor(f"in_{k}", v.shape, mybir.dt.from_np(v.dtype), kind="ExternalInput").ap()
         for k, v in arrays.items()}
    out = nc.dram_tensor("out_0", [NP, F], F32, kind="ExternalOutput").ap()
    build(nc, A, out)
    r = run_bass_kernel_spmd(nc, [{f"in_{k}": v for k, v in arrays.items()}], core_ids=[0])
    return np.ascontiguousarray(r.results[0]["out_0"][:N])
```

```python
import numpy as np
import concourse.bass as bass
from concourse import mybir
from contextlib import ExitStack

F32 = mybir.dt.float32
I32 = mybir.dt.int32
I16 = mybir.dt.int16
BF16 = mybir.dt.bfloat16
ALU = mybir.AluOpType
ACT = mybir.ActivationFunctionType
AX = mybir.AxisListType

N, E, F, H, C, ED = 6250, 200000, 256, 8, 32, 16
P = 128
HX = C + 1
ROW = H * HX
MSG = ROW + H + 1
WINDOWS = -(-N // P)
TILES = WINDOWS + WINDOWS % 2
PAIRS = TILES // 2
CHUNKS = max(c for c in range(1, 6) if PAIRS % c == 0)
NP = TILES * P
STEP = 512
J = STEP // P
S = 4
SLOTS = 3
STEPS = -(-(-(-E // STEP) + WINDOWS) // S) * S
MACROS = STEPS // S
ROUNDS = (MACROS - 3) // SLOTS
EP = E + 2 * STEP
NO_NODE = 1 << 14
CP = 125
CC = E // CP
FF = 4 * F
FT = FF // P
KT = F // P
BIG = 1e30
VB1, VB2, VBIAS, VG1, VE1, VG2, VE2, VFB2 = range(8)


class Chain:

    def __init__(self, sem):
        self.sem, self.base, self.k, self.it, self.per = sem, 0, 0, None, 0

    def enter(self, it, first, per):
        self.base += self.k - first * per
        self.k, self.it, self.per = 0, it, per

    def leave(self, end):
        assert self.k == self.per, (self.k, self.per)
        self.base += end * self.per
        self.k, self.it, self.per = 0, None, 0

    def inc(self, ins):
        ins.then_inc(self.sem, 1)
        self.k += 1
        return self.k

    def wait(self, eng, k=None):
        k = self.k if k is None else k
        eng.wait_ge(self.sem, self.base + k if self.it is None else self.it * self.per + (self.base + k))


def build(nc, A, out):
    with ExitStack() as ctx:
        def sb(name, shape, dt=F32):
            return ctx.enter_context(nc.sbuf_tensor(name, shape, dt))

        def phase(run, *args):
            sems = []

            def sem(name):
                sems.append(nc.alloc_semaphore(name=name))
                return sems[-1]
            run(nc, sem, *args)
            nc.clear_and_free_semaphores(sems)
            nc.all_engine_barrier()

        htab = [nc.dram_tensor(f"htab{l}", [NP, ROW], F32).ap() for l in range(3)]
        x1_dram = nc.dram_tensor("x1_dram", [NP, F], F32).ap()
        res_dram = nc.dram_tensor("res_dram", [NP, F], F32).ap()
        link_dram = nc.dram_tensor("link_dram", [EP], F32).ap()

        m = {}
        m["acc"] = sb("acc", [P, TILES, H, HX])
        m["acc_max"] = sb("acc_max", [P, TILES, H])
        m["a_dst"] = sb("a_dst", [P, TILES, H])
        m["a_dst3"] = sb("a_dst3", [P, TILES, 3, H], BF16)
        m["ident"] = sb("ident", [P, P])
        m["iota"] = sb("iota", [P, P])
        m["pidx"] = sb("pidx", [P, 1])
        m["last_row"] = sb("last_row", [P, S, J])
        m["w_base"] = sb("w_base", [P, STEPS])
        m["w_of"] = sb("w_of", [1, STEPS], I32)
        m["e_of"] = sb("e_of", [1, STEPS], I32)
        m["wx"] = [sb(f"wx{l}", [P, KT, ROW + H]) for l in range(3)]
        m["wres"] = sb("wres", [P, KT, F])
        m["webd"] = sb("webd", [S * ED, 2, S, H])
        m["vec"] = sb("vec", [P, 8, F])
        m["fb1"] = sb("fb1", [P, FT])
        m["gbuf"] = sb("gbuf", [P, SLOTS, S, J, MSG])
        m["onehot"] = sb("onehot", [P, SLOTS, S * J, P])
        m["onehot_t"] = sb("onehot_t", [P, SLOTS, S, STEP], BF16)
        m["dst_all"] = sb("dst_all", [P, S, STEP], I32)
        m["ea"] = sb("ea", [S * ED, SLOTS, STEP])
        m["rec"] = sb("rec", [P, SLOTS, S, J, 4], I32)
        psum = ctx.enter_context(nc.psum_tensor("psum", [P, 8, 512], F32))

        phase(setup, A, m, psum, link_dram)
        for l in range(3):
            phase(nodes_in, A, m, psum, l, htab, x1_dram, res_dram)
            phase(edges, A, m, psum, l, htab, link_dram)
        phase(nodes_out, A, m, psum, x1_dram, res_dram, out)


def scratch(m, sizes, where="gbuf"):
    if where == "gbuf":
        flat = m["gbuf"][:, :, :, :, :].rearrange("p a b c d -> p (a b c d)")
    else:
        flat = m["onehot"][:, :, :, :].rearrange("p a b c -> p (a b c)")
    at, got = 0, {}
    for name, shape in sizes.items():
        n = int(np.prod(shape))
        v = flat[:, at:at + n]
        if len(shape) == 2:
            v = v.rearrange("p (a b) -> p a b", a=shape[0])
        elif len(shape) == 3:
            v = v.rearrange("p (a b c) -> p a b c", a=shape[0], b=shape[1])
        got[name] = v
        at += n
    assert at <= SLOTS * S * J * (MSG if where == "gbuf" else P), at
    return got


def setup(nc, sem, A, m, psum, link_dram):
    v = scratch(m, {"w_raw": (3, KT, F), "att": (8, F), "prod": (KT, F), "we_raw": (2, F),
                    "we": (2, H), "mask": (S, H), "ones": (P,), "thr": (1,), "istep": (STEPS,),
                    "cnt": (WINDOWS,), "diff": (WINDOWS,), "tri": (WINDOWS,), "size": (1,), "steps": (1,),
                    "coef": (1,), "coef_b": (P,), "first": (1,), "tmp": (1,)})
    reached = m["onehot"][:, 2, :, :].rearrange("p a b -> p (a b)")[:, 0:STEPS]
    dst_raw = m["onehot"][0:CP, 0, :, :].rearrange("p a b -> p (a b)").bitcast(I32)[:, 0:CC]
    dst_16 = m["onehot"][0:CP, 1, :, :].rearrange("p a b -> p (a b)").bitcast(I16)[:, 0:CC]
    junk_16 = m["onehot_t"][0:CP, 0, :, :].rearrange("p a b -> p (a b)").bitcast(I16)[:, 0:CC]
    dst_next = m["dst_all"][0:CP, :, :].rearrange("p a b -> p (a b)")[:, 0:CC]
    link = m["onehot_t"][0:CP, 1:3, :, :].rearrange("p a b c -> p (a b c)").bitcast(F32)[:, 0:CC]
    edge_links = m["rec"][0:1, :, :, :, :].rearrange("p a b c d -> p (a b c d)").bitcast(F32)
    ints = m["dst_all"][0:WINDOWS, 0, 0:2]
    next_in, link_ready, link_out = sem("next_in"), sem("link_ready"), sem("link_out")
    dst_in, w_in, const, ps_done = sem("dst_in"), sem("w_in"), sem("const"), sem("setup_pe")
    dv, pool_own = sem("setup_dve"), sem("setup_pool")
    to_pe = sem("setup_to_pe")

    with nc.Block() as block:
        @block.sync
        def _(sp):
            sp.dma_start(dst_raw, A["dst"][0:E].rearrange("(p c) -> p c", p=CP)).then_inc(dst_in, 16)
            sp.dma_start(dst_next, A["dst"][1:E + 1].rearrange("(p c) -> p c", p=CP)).then_inc(next_in, 16)
            for l, w in enumerate(("L0_gnn_W1", "L0_gnn_W2", "L1_gnn_W")):
                sp.dma_start(v["w_raw"][:, l, :, :], A[w].rearrange("(k p) c -> p k c", p=P)).then_inc(w_in, 16)
            atts = ("L0_gnn_att_src1", "L0_gnn_att_dst1", "L0_gnn_att_src2", "L0_gnn_att_dst2",
                    "L1_gnn_att_src", "L1_gnn_att_dst", "L0_gnn_att_e1", "L0_gnn_att_e2")
            for i, a in enumerate(atts):
                sp.dma_start(v["att"][:, i, :], A[a].rearrange("h c -> (h c)").partition_broadcast(P)).then_inc(w_in, 16)
            for l, w in enumerate(("L0_gnn_W_e1", "L0_gnn_W_e2")):
                for s in range(S):
                    sp.dma_start(v["we_raw"][ED * s:ED * s + ED, l, :], A[w]).then_inc(w_in, 16)
            sp.dma_start(m["wres"][:, :, :], A["L1_gnn_W_res"].rearrange("(k p) c -> p k c", p=P)).then_inc(w_in, 16)
            vecs = ("L0_gnn_b1", "L0_gnn_b2", "L1_gnn_bias", "L1_gnn_ln1_g", "L1_gnn_ln1_b", "L1_gnn_ln2_g",
                    "L1_gnn_ln2_b", "L1_gnn_ffn_b2")
            for i, a in enumerate(vecs):
                sp.dma_start(m["vec"][:, i, :], A[a].partition_broadcast(P)).then_inc(w_in, 16)
            sp.dma_start(m["fb1"][:, :], A["ffn_b1_cols"]).then_inc(w_in, 16)
            sp.wait_ge(link_ready, 1)
            sp.dma_start(link_dram[1:E + 1].rearrange("(p c) -> p c", p=CP), link).then_inc(link_out, 16)
            sp.dma_start(link_dram[0:1].rearrange("(a n) -> a n", a=1), edge_links[:, 0:1]).then_inc(link_out, 16)
            rest, at = EP - E - 1, E + 1
            while rest:
                n = min(rest, SLOTS * S * J * 4)
                sp.dma_start(link_dram[at:at + n].rearrange("(a n) -> a n", a=1), edge_links[:, 0:n]
                             ).then_inc(link_out, 16)
                rest, at = rest - n, at + n
            sp.wait_ge(link_out, 16 * (2 + -(-(EP - E - 1) // (SLOTS * S * J * 4))))
            sp.wait_ge(w_in, 16 * (3 + 8 + 2 * S + 1 + 8 + 1))

        @block.gpsimd
        def _(pool):
            def own(ins, n=[0]):
                n[0] += 1
                ins.then_inc(pool_own, 1)
                pool.wait_ge(pool_own, n[0])
            own(pool.memset(m["ident"][:, :], 0.0))
            own(pool.affine_select(out=m["ident"][:, :], in_=m["ident"][:, :], compare_op=ALU.not_equal, fill=1.0,
                                   base=0, pattern=[[-1, P]], channel_multiplier=1))
            own(pool.iota(m["iota"][:, :], pattern=[[1, P]], base=0, channel_multiplier=0,
                          allow_small_or_imprecise_dtypes=True))
            own(pool.iota(m["pidx"][:, :], pattern=[[0, 1]], base=0, channel_multiplier=1,
                          allow_small_or_imprecise_dtypes=True))
            own(pool.iota(v["istep"], pattern=[[1, STEPS]], base=0, channel_multiplier=0,
                          allow_small_or_imprecise_dtypes=True))
            own(pool.memset(v["ones"], 1.0))
            own(pool.memset(v["tri"], 1.0))
            own(pool.affine_select(out=v["tri"], in_=v["tri"], compare_op=ALU.is_ge, fill=0.0,
                                   base=0, pattern=[[1, WINDOWS]], channel_multiplier=-1))
            own(pool.memset(m["last_row"][:, :, :], 0.0))
            own(pool.affine_select(out=m["last_row"][:, :, :], in_=m["last_row"][:, :, :], compare_op=ALU.not_equal,
                                   fill=1.0, base=-(J * P - 1), pattern=[[0, S], [1, J]], channel_multiplier=J))
            own(pool.memset(v["mask"], 1.0))
            own(pool.affine_select(out=v["mask"], in_=v["mask"], compare_op=ALU.is_ge, fill=0.0,
                                   base=0, pattern=[[-ED, S], [0, H]], channel_multiplier=1))
            own(pool.affine_select(out=v["mask"], in_=v["mask"], compare_op=ALU.is_ge, fill=0.0,
                                   base=ED - 1, pattern=[[ED, S], [0, H]], channel_multiplier=-1))
            pool.memset(m["acc_max"][:, :, :], -BIG).then_inc(const, 1)
            pool.memset(m["acc"][:, :, :, :], 0.0).then_inc(const, 1)

        @block.vector
        def _(dve):
            ch = Chain(dv)
            V = nc.vector
            cnt, diff = v["cnt"][0:CP, :], v["diff"][0:CP, :]
            dve.wait_ge(dst_in, 16)
            dve.wait_ge(next_in, 16)
            ch.inc(V.memset(edge_links, -BIG))
            ch.inc(V.tensor_tensor(link, dst_raw, dst_next, ALU.is_equal))
            ch.wait(dve)
            V.tensor_scalar(link, link, 1.0, BIG, ALU.subtract, ALU.mult).then_inc(link_ready, 1)
            ch.inc(V.tensor_copy(dst_16, dst_raw))
            ch.inc(V.memset(cnt[:, 0:1], 0.0))
            ch.inc(V.memset(diff[:, 0:1], 0.0))
            ch.wait(dve)
            for w in range(1, WINDOWS):
                ch.inc(V.tensor_scalar(junk_16, dst_16, float(P * w), 0.0, ALU.is_lt, ALU.add,
                                       accum_out=cnt[:, w:w + 1]))
                ch.wait(dve)
            ch.inc(V.tensor_tensor(diff[:, 1:WINDOWS], cnt[:, 1:WINDOWS], cnt[:, 0:WINDOWS - 1], ALU.subtract))
            dve.wait_ge(const, 2)
            V.tensor_copy(v["tmp"], v["ones"][:, 0:1]).then_inc(to_pe, 1)
            dve.wait_ge(to_pe, 1)
            dve.wait_ge(ps_done, 1)
            size, steps = v["size"][0:WINDOWS, :], v["steps"][0:WINDOWS, :]
            ch.inc(V.tensor_copy(size, psum[0:WINDOWS, 0, 0:1]))
            ch.inc(V.tensor_scalar(ints[:, 0:1], psum[0:WINDOWS, 0, 0:1], float(STEP - 1), None, ALU.add))
            ch.wait(dve)
            ch.inc(V.tensor_scalar(ints[:, 1:2], ints[:, 0:1], STEP.bit_length() - 1, None, ALU.arith_shift_right))
            ch.wait(dve)
            ch.inc(V.tensor_copy(steps, ints[:, 1:2]))
            ch.wait(dve)
            ch.inc(V.scalar_tensor_tensor(v["coef"][0:WINDOWS, :], steps, -float(STEP), size, ALU.mult, ALU.add))
            ch.wait(dve)
            V.tensor_scalar(v["coef_b"][0:WINDOWS, :], v["ones"][0:WINDOWS, :], v["coef"][0:WINDOWS, 0:1], None,
                            ALU.mult).then_inc(to_pe, 1)
            dve.wait_ge(ps_done, 2)
            ch.inc(V.tensor_copy(v["first"][0:WINDOWS, :], psum[0:WINDOWS, 1, 0:1]))
            ch.wait(dve)
            V.tensor_scalar(reached[0:WINDOWS, :], v["istep"][0:WINDOWS, :], v["first"][0:WINDOWS, 0:1], None,
                            ALU.is_ge).then_inc(to_pe, 1)
            dve.wait_ge(ps_done, 3)
            ch.inc(V.tensor_scalar(m["w_base"][:, :], psum[:, 3, 0:STEPS], 1.0, float(P), ALU.subtract, ALU.mult))
            ch.inc(V.tensor_scalar(m["w_of"][:, :], psum[0:1, 3, 0:STEPS], 1.0, None, ALU.subtract))
            first_edge = m["onehot"][0:1, 2, 8:16, :].rearrange("p a b -> p (a b)")[:, 0:STEPS]
            ch.inc(V.scalar_tensor_tensor(first_edge, v["istep"][0:1, :], float(STEP), psum[0:1, 2, 0:STEPS],
                                          ALU.mult, ALU.add))
            ch.wait(dve)
            ch.inc(V.tensor_scalar(m["e_of"][:, :], first_edge, float(E), None, ALU.min))
            dve.wait_ge(w_in, 16 * (3 + 8 + 2 * S + 1 + 8 + 1))
            for l in range(3):
                for k in range(KT):
                    raw = v["w_raw"][:, l, k, :]
                    heads = m["wx"][l][:, k, 0:ROW].rearrange("p (h x) -> p h x", x=HX)
                    ch.inc(V.tensor_copy(heads[:, :, 0:C], raw.rearrange("p (h c) -> p h c", c=C)))
                    for d in range(2):
                        ch.inc(V.tensor_tensor(v["prod"][:, d, :], raw, v["att"][:, 2 * l + d, :], ALU.mult))
                        ch.wait(dve)
                        to = heads[:, :, C:HX].rearrange("p h o -> p (h o)") if d == 0 else m["wx"][l][:, k, ROW:ROW + H]
                        ch.inc(V.reduce_sum(to, v["prod"][:, d, :].rearrange("p (h c) -> p h c", c=C), axis=AX.X))
                        ch.wait(dve)
            K = S * ED
            for l in range(2):
                ch.inc(V.tensor_tensor(v["prod"][0:K, l, :], v["we_raw"][0:K, l, :], v["att"][0:K, 6 + l, :], ALU.mult))
                ch.wait(dve)
                ch.inc(V.reduce_sum(v["we"][0:K, l, :], v["prod"][0:K, l, :].rearrange("p (h c) -> p h c", c=C),
                                    axis=AX.X))
                ch.wait(dve)
                ch.inc(V.tensor_tensor(m["webd"][:, l, :, :], v["mask"][0:K, :, :],
                                       v["we"][0:K, l, :].unsqueeze(1).to_broadcast([K, S, H]), ALU.mult))

        @block.tensor
        def _(pe):
            T = nc.tensor
            pe.wait_ge(to_pe, 1)
            T.matmul(psum[0:WINDOWS, 0, 0:1], v["diff"][0:CP, :], v["ones"][0:CP, 0:1]).then_inc(ps_done, 1)
            pe.wait_ge(to_pe, 2)
            T.matmul(psum[0:WINDOWS, 1, 0:1], v["tri"][0:WINDOWS, :], v["steps"][0:WINDOWS, :]).then_inc(ps_done, 1)
            pe.wait_ge(to_pe, 3)
            T.matmul(psum[:, 2, 0:STEPS], v["coef_b"][0:WINDOWS, :], reached[0:WINDOWS, :])
            T.matmul(psum[:, 3, 0:STEPS], v["ones"][0:WINDOWS, :], reached[0:WINDOWS, :]).then_inc(ps_done, 1)


def load_pair(dram, i):
    return dram[bass.ds(i * (2 * P), 2 * P), :].rearrange("(b p) c -> p b c", p=P)


def is_later(i):
    return not isinstance(i, int) or i > 0


def pairs(eng, body):
    body(0)
    with eng.Fori(1, PAIRS - 1) as i:
        body(i)
    body(PAIRS - 1)


def has_next(i):
    return not isinstance(i, int) or i < PAIRS - 1


def nodes_in(nc, sem, A, m, psum, l, htab, x1_dram, res_dram):
    v = scratch(m, {"x_all": (TILES, F)}) if l == 0 else {}
    v.update(scratch(m, {"x_in": (2, F), "h_in": (2, F), "h_t": (2, KT, P), "row": (2, ROW), "den": (2, H),
                    "y": (2, F), "stat": (2, 6), "mv": (2, 2), "rstd": (2, 1), "mv2": (2, 2), "rstd2": (2, 1),
                    "x2b": (2, F), "xn": (2, F), "res": (2, F), "self": (2, H), "zeros": (2, ROW), "eps": (1,)},
                     "onehot" if l == 0 else "gbuf"))
    n = f"_n{l}"
    chunk_in = [sem(f"x_in{c}" + n) for c in range(CHUNKS if l == 0 else 0)]
    (x_in, row_out, x1_out, res_out, x_used, act_ready, h_tr, h_t_ready, proj, row_ready, proj_used, own, x1_ready,
     var_ready, std_ready, res_ready, pre_ready) = (
        sem(k + n) for k in ("x_in", "row_out", "x1_out", "res_out", "x_used", "act_ready", "h_tr", "h_t_ready",
                             "proj", "row_ready", "proj_used", "dve", "x1_ready", "var_ready", "std_ready",
                             "res_ready", "pre_ready"))

    with nc.Block() as block:
        def store_rows(eng, i):
            eng.wait_ge(row_ready, i + 1)
            eng.nop(nofuse=True)
            eng.dma_start(load_pair(htab[l], i), v["row"]).then_inc(row_out, 16)

        @block.sync
        def _(sp):
            def body(i):
                if l == 2 and has_next(i):
                    sp.wait_ge(x_used, i + 1)
                    sp.nop(nofuse=True)
                    sp.dma_start(v["x_in"], load_pair(A["x"], i + 1)).then_inc(x_in, 16)
                if l == 2:
                    sp.wait_ge(x1_ready, i + 1)
                    sp.nop(nofuse=True)
                    sp.dma_start(load_pair(x1_dram, i), v["y"]).then_inc(x1_out, 16)
                else:
                    store_rows(sp, i)
            if l == 0:
                n = TILES // CHUNKS
                for c in range(CHUNKS):
                    sp.dma_start(v["x_all"][:, c * n:(c + 1) * n, :],
                                 A["x"][c * n * P:(c + 1) * n * P, :].rearrange("(t p) c -> p t c", p=P)
                                 ).then_inc(chunk_in[c], 16)
            if l == 2:
                sp.dma_start(v["x_in"], load_pair(A["x"], 0)).then_inc(x_in, 16)
            pairs(sp, body)
            sp.wait_ge(x1_out if l == 2 else row_out, 16 * PAIRS)
            sp.nop(nofuse=True)

        @block.gpsimd
        def _(pool):
            if l == 0:
                for c in range(CHUNKS):
                    pool.wait_ge(chunk_in[c], 16)
                    pool.sem_inc(x_in, PAIRS // CHUNKS)
            if l != 2:
                return

            def body(i):
                pool.wait_ge(res_ready, i + 1)
                pool.nop(nofuse=True)
                pool.dma_start(load_pair(res_dram, i), v["res"]).then_inc(res_out, 16)
                store_rows(pool, i)
            pairs(pool, body)
            pool.wait_ge(res_out, 16 * PAIRS)
            pool.wait_ge(row_out, 16 * PAIRS)

        @block.scalar
        def _(act):
            def activations(i):
                if l == 0:
                    act.wait_ge(x_in, i + 1)
                    src = v["x_all"][:, bass.ds(i * 2, 2), :]
                else:
                    act.wait_ge(pre_ready, i + 1)
                    src = v["y"]
                nc.scalar.activation(v["h_in"], src, ACT.Relu).then_inc(act_ready, 1)

            def deviations(i, q):
                act.wait_ge(var_ready, i * 2 + (q + 1))
                mv, rs = (v["mv"], v["rstd"]) if q == 0 else (v["mv2"], v["rstd2"])
                nc.scalar.activation(rs, mv[:, :, 1:2], ACT.Sqrt, bias=v["eps"][:, 0:1]).then_inc(std_ready, 1)

            def body(i):
                for b in range(2):
                    act.wait_ge(h_tr, i * 2 + (b + 1))
                    if is_later(i):
                        act.wait_ge(proj, i * 2 + (b - 1))
                    nc.scalar.activation(v["h_t"][:, b, :, :], psum[:, b, 0:F].rearrange("p (k n) -> p k n", k=KT),
                                         ACT.Copy).then_inc(h_t_ready, 1)
                if has_next(i):
                    if l < 2:
                        activations(i + 1)
                    else:
                        deviations(i + 1, 0)
                        deviations(i + 1, 1)
                act.wait_ge(proj, i * 2 + 2)
                if is_later(i):
                    act.wait_ge(row_out, i * 16)
                nc.scalar.activation(v["row"], psum[:, 2:4, 0:ROW], ACT.Copy).then_inc(row_ready, 1)
            act.wait_ge(own, 1)
            if l < 2:
                activations(0)
            else:
                deviations(0, 0)
                deviations(0, 1)
            pairs(act, body)

        @block.tensor
        def _(pe):
            def body(i):
                pe.wait_ge(act_ready, i + 1)
                for b in range(2):
                    if is_later(i):
                        pe.wait_ge(h_t_ready, i * 2 + (b - 1))
                    for k in range(KT):
                        last = nc.tensor.transpose(psum[:, b, k * P:(k + 1) * P],
                                                   v["h_in"][:, b, k * P:(k + 1) * P], m["ident"][:, :])
                    last.then_inc(h_tr, 1)
                for b in range(2):
                    pe.wait_ge(h_t_ready, i * 2 + (b + 1))
                    if b == 0 and is_later(i):
                        pe.wait_ge(row_ready, i)
                        pe.wait_ge(proj_used, i)
                    for k in range(KT):
                        last = nc.tensor.matmul(psum[:, 2 + b, 0:ROW + H], v["h_t"][:, b, k, :],
                                                m["wx"][l][:, k, :], start=k == 0, stop=k == KT - 1)
                    if l == 2:
                        for k in range(KT):
                            last = nc.tensor.matmul(psum[:, 4 + b, 0:F], v["h_t"][:, b, k, :], m["wres"][:, k, :],
                                                    start=k == 0, stop=k == KT - 1)
                    last.then_inc(proj, 1)
            pairs(pe, body)

        @block.vector
        def _(dve):
            ch = Chain(own)
            V = nc.vector

            def heads(i):
                return m["acc"][:, bass.ds(i * 2, 2), :, :].rearrange("p b h x -> p (b h) x")

            def maxima(i):
                return m["acc_max"][:, bass.ds(i * 2, 2), :]

            def on_both(row):
                return m["vec"][:, row, :].unsqueeze(1).to_broadcast([P, 2, F])

            def normalised(i):
                acc, den = heads(i), v["den"].rearrange("p b h -> p (b h)")
                ch.inc(V.tensor_scalar(den, acc[:, :, C:HX].rearrange("p h o -> p (h o)"), 1e-16, None, ALU.add))
                ch.wait(dve)
                ch.inc(V.reciprocal(den, den))
                ch.wait(dve)
                if l == 1 and is_later(i):
                    dve.wait_ge(act_ready, i)
                if l == 2 and is_later(i):
                    dve.wait_ge(x1_out, i * 16)
                ch.inc(V.tensor_tensor(v["y"].rearrange("p b (h c) -> p (b h) c", c=C), acc[:, :, 0:C],
                                       den.unsqueeze(2).to_broadcast([P, 2 * H, C]), ALU.mult))
                ch.wait(dve)

            def stats(src, mv):
                for b in range(2):
                    ch.inc(V.bn_stats(v["stat"][:, b, :], src[:, b, :]))
                ch.wait(dve)
                dve.nop(nofuse=True)
                V.bn_aggr(v[mv][:, 0, :], v["stat"][:, 0, :])
                V.bn_aggr(v[mv][:, 1, :], v["stat"][:, 1, :]).then_inc(var_ready, 1)

            def standardised(out, src, mv, rs, i, q):
                dve.wait_ge(std_ready, i * 2 + (q + 1))
                ch.inc(V.reciprocal(v[rs], v[rs]))
                ch.wait(dve)
                for b in range(2):
                    ch.inc(V.tensor_scalar(out[:, b, :], src[:, b, :], v[mv][:, b, 0:1], v[rs][:, b, 0:1],
                                           ALU.subtract, ALU.mult))
                ch.wait(dve)

            def before(i):
                normalised(i)
                V.tensor_tensor(v["y"], v["y"], on_both(VB1), ALU.add).then_inc(pre_ready, 1)
                ch.inc(V.tensor_copy(heads(i).rearrange("p h x -> p (h x)"), v["zeros"].rearrange("p b c -> p (b c)")))
                ch.inc(V.tensor_scalar(maxima(i), v["zeros"][:, :, 0:H], -BIG, None, ALU.add))

            def logits_out(i):
                dve.wait_ge(proj, i * 2 + 2)
                dve.wait_ge(row_ready, i + 1)
                to = m["a_dst"][:, bass.ds(i * 2, 2), :]
                ch.inc(V.tensor_copy(to, psum[:, 2:4, ROW:ROW + H]))
                if l == 2:
                    acc = m["acc"][:, bass.ds(i * 2, 2), :, :].rearrange("p b h x -> p b (h x)")
                    ch.inc(V.tensor_copy(acc, psum[:, 2:4, 0:ROW]))
                    if is_later(i):
                        dve.wait_ge(res_out, i * 16)
                    V.tensor_tensor(v["res"], psum[:, 4:6, 0:F], on_both(VBIAS), ALU.add).then_inc(res_ready, 1)
                    ch.wait(dve)
                    a_src = heads(i)[:, :, C:HX].rearrange("p h o -> p (h o)")
                    e = v["self"].rearrange("p b h -> p (b h)")
                    ch.inc(V.tensor_tensor(e, a_src, to.rearrange("p b h -> p (b h)"), ALU.add))
                    ch.wait(dve)
                    ch.inc(V.scalar_tensor_tensor(maxima(i).rearrange("p b h -> p (b h)"), e, 0.2, e, ALU.mult,
                                                  ALU.max))
                    ch.inc(V.tensor_scalar(a_src, v["zeros"][:, 0, 0:2 * H], 1.0, None, ALU.add))
                    dve.wait_ge(res_ready, i + 1)
                ch.wait(dve)
                dve.sem_inc(proj_used, 1)

            def first_norm(i):
                dve.wait_ge(x_in, i * 16 + 16)
                V.scalar_tensor_tensor(v["x2b"], v["x_in"], 2.0, on_both(VB2), ALU.mult, ALU.add).then_inc(x_used, 1)
                normalised(i)
                dve.wait_ge(x_used, i + 1)
                ch.inc(V.tensor_tensor(v["y"], v["y"], v["x2b"], ALU.add))
                ch.wait(dve)
                stats(v["y"], "mv")

            def second_norm(i):
                standardised(v["y"], v["y"], "mv", "rstd", i, 0)
                dve.sem_inc(x1_ready, 1)
                stats(v["y"], "mv2")

            def affine(i):
                xn = v["xn"]
                standardised(xn, v["y"], "mv2", "rstd2", i, 1)
                ch.inc(V.tensor_tensor(xn, xn, on_both(VG1), ALU.mult))
                ch.wait(dve)
                if is_later(i):
                    dve.wait_ge(h_tr, i * 2)
                V.tensor_tensor(v["h_in"], xn, on_both(VE1), ALU.add).then_inc(act_ready, 1)

            def body(i):
                if has_next(i):
                    if l == 1:
                        before(i + 1)
                    elif l == 2:
                        first_norm(i + 1)
                        second_norm(i + 1)
                        affine(i + 1)
                logits_out(i)

            ch.inc(V.memset(v["eps"], 1e-5))
            ch.inc(V.memset(v["zeros"], 0.0))
            ch.wait(dve)
            if l == 1:
                before(0)
            elif l == 2:
                first_norm(0)
                second_norm(0)
                affine(0)
            k0 = ch.k
            body(0)
            per = ch.k - k0
            with dve.Fori(1, PAIRS - 1) as i:
                ch.enter(i, 1, per)
                body(i)
                ch.leave(PAIRS - 1)
            body(PAIRS - 1)
            ch.wait(dve)


def edges(nc, sem, A, m, psum, l, htab, link_dram):
    n = f"_e{l}"
    has_ea = l < 2
    rec_in = [sem(f"rec_in{k}" + n) for k in range(SLOTS)]
    gathered = [sem(f"gathered{k}" + n) for k in range(SLOTS)]
    link_in = [sem(f"link_in{k}" + n) for k in range(SLOTS)]
    ea_in = [sem(f"ea_in{k}" + n) for k in range(SLOTS)]
    (dst_all_in, split_ready, nid_ready, rec_used, onehot_t_ready, onehot_ready, pre_ready, alpha_ready, alpha_t,
     alpha_t_sb, max_ready, max_back, max_used, diff_ready, exp_ready, weighted, summed, merged, rescale_ready,
     rescaled, own, act_own) = (
        sem(k + n) for k in ("dst_all_in", "split_ready", "nid_ready", "rec_used", "onehot_t_ready", "onehot_ready",
                             "pre_ready", "alpha_ready", "alpha_t", "alpha_t_sb", "max_ready", "max_back", "max_used",
                             "diff_ready", "exp_ready", "weighted", "summed", "merged", "rescale_ready", "rescaled",
                             "dve", "act"))
    gbuf, rec, onehot, onehot_t = m["gbuf"], m["rec"], m["onehot"], m["onehot_t"]
    psA = psum[:, 0, 0:J * S * H]
    psT = psum[0:S * H, 1, :]
    psR = psum[:, 2, 0:J * S * H]
    psM = psum[:, 4:8, :]

    with ExitStack() as ctx:
        def sb(name, shape, dt=F32):
            return ctx.enter_context(nc.sbuf_tensor(name + n, shape, dt))
        w4 = sb("w4", [P, SLOTS, S])
        nid4 = sb("nid4", [P, SLOTS, S])
        dl = sb("dl", [P, SLOTS, S, J])
        flag = sb("flag", [P, SLOTS, S, J])
        alpha = sb("alpha", [P, J, S * H])
        asum = sb("asum", [P, J, S * H])
        dif = sb("dif", [P, J, S * H])
        aT = sb("aT", [S * H, STEP])
        fwd = sb("fwd", [S * H, STEP])
        mx = sb("mx", [S * H, STEP])
        link = sb("link", [S * H, SLOTS, STEP + 1])
        part_max = sb("part_max", [P, S, H])
        untouched = sb("untouched", [P, S])
        old_max = sb("old_max", [P, S, H])
        new_max = sb("new_max", [P, S, H])
        d12 = sb("d12", [P, 2, S, H])
        r12 = sb("r12", [P, 2, S, H])
        part = sb("part", [P, S, H, HX])

        def rounds(eng, body, chain=None, per=0):
            for k in range(SLOTS):
                body(0, k)
            with eng.Fori(1, ROUNDS) as i:
                if chain:
                    chain.enter(i, 1, per)
                for k in range(SLOTS):
                    body(i, k)
                if chain:
                    chain.leave(ROUNDS)
            for M in range(ROUNDS * SLOTS, MACROS):
                body(M // SLOTS, M % SLOTS)

        def has(i, k, d):
            return not isinstance(i, int) or 0 <= SLOTS * i + k + d < MACROS

        def ahead(i, k, d):
            return (i + (k + d) // SLOTS, (k + d) % SLOTS)

        def windows_of(eng, M, macros=1):
            _, w = nc.values_load_multi_w_load_instructions(m["w_of"][0:1, bass.ds(M * S, macros * S)],
                                                            engines=[eng], min_val=0, max_val=WINDOWS - 1)
            return w

        with nc.Block() as block:
            @block.sync
            def _(sp):
                def body(i, k):
                    M = i * SLOTS + k
                    _, at = nc.values_load_multi_w_load_instructions(
                        m["e_of"][0:1, bass.ds(M * S, S)], engines=[mybir.EngineType.SP], min_val=0, max_val=E)
                    if has(i, k, -SLOTS):
                        sp.wait_ge(gathered[k], i * (16 * S * J))
                        sp.nop(nofuse=True)
                        sp.wait_ge(rec_used, M - (SLOTS - 1))
                        sp.nop(nofuse=True)
                    for s in range(S):
                        sp.dma_start(rec[:, k, s, :, :].rearrange("p j f -> p (j f)"),
                                     A["records"][bass.ds(at[s], STEP), :].rearrange("(p j) f -> p (j f)", j=J)
                                     ).then_inc(rec_in[k], 16)
                    if has(i, k, -1):
                        sp.wait_ge(onehot_t_ready, M)
                        sp.nop(nofuse=True)
                    for s in range(S):
                        sp.dma_start(m["dst_all"][:, s, :], A["dst"][bass.ds(at[s], STEP)].partition_broadcast(P)
                                     ).then_inc(dst_all_in, 16)
                    if has_ea:
                        if has(i, k, -SLOTS):
                            sp.wait_ge(pre_ready, M - (SLOTS - 1))
                            sp.nop(nofuse=True)
                        for s in range(S):
                            sp.dma_start(m["ea"][ED * s:ED * s + ED, k, :], A["ea_t"][:, bass.ds(at[s], STEP)]
                                         ).then_inc(ea_in[k], 16)
                    if has(i, k, -SLOTS):
                        sp.wait_ge(max_ready, M - (SLOTS - 1))
                        sp.nop(nofuse=True)
                    for s in range(S):
                        sp.dma_start(link[H * s:H * s + H, k, :],
                                     link_dram[bass.ds(at[s], STEP + 1)].partition_broadcast(H)
                                     ).then_inc(link_in[k], 16)
                rounds(sp, body)

            @block.gpsimd
            def _(pool):
                def body(i, k):
                    M = i * SLOTS + k
                    pool.wait_ge(rec_in[k], i * (16 * S) + 16 * S)
                    if has(i, k, -SLOTS):
                        pool.wait_ge(summed, (M - (SLOTS - 1)) * S)
                    pool.nop(nofuse=True)
                    for s in range(S):
                        for j in range(J):
                            pool.indirect_dma_start(
                                out=gbuf[:, k, s, j, 0:ROW], out_offset=None, in_=htab[l],
                                in_offset=bass.IndirectOffsetOnAxis(ap=rec[:, k, s, j, 0:1], axis=0),
                            ).then_inc(gathered[k], 16)
                rounds(pool, body)

            @block.scalar
            def _(act):
                ch = Chain(act_own)
                G = nc.scalar

                def edge_onehot(i, k, M):
                    act.wait_ge(rec_used, M + 1)
                    if has(i, k, -SLOTS):
                        act.wait_ge(summed, (M - (SLOTS - 1)) * S)
                    for s in range(S):
                        for j in range(J):
                            last = G.activation(onehot[:, k, s * J + j, :], m["iota"][:, :], ACT.Abs,
                                                bias=dl[:, k, s, j:j + 1])
                    ch.inc(last)
                    ch.wait(act)
                    G.activation(onehot[:, k, :, :], onehot[:, k, :, :], ACT.Relu, bias=1.0, scale=-1.0
                                 ).then_inc(onehot_ready, 1)

                def distances(i, k, M):
                    act.wait_ge(nid_ready, M + 1)
                    act.wait_ge(dst_all_in, M * (16 * S) + 16 * S)
                    if has(i, k, -SLOTS):
                        act.wait_ge(pre_ready, M - (SLOTS - 1))
                    for s in range(S):
                        last = G.activation(onehot_t[:, k, s, :], m["dst_all"][:, s, :], ACT.Abs,
                                            bias=nid4[:, k, s:s + 1])
                    ch.inc(last)

                def transposed_onehot(k):
                    ch.wait(act)
                    G.activation(onehot_t[:, k, :, :], onehot_t[:, k, :, :], ACT.Relu, bias=1.0, scale=-1.0
                                 ).then_inc(onehot_t_ready, 1)

                def rescale(M):
                    act.wait_ge(rescale_ready, M + 1)
                    G.activation(r12[:, :, :, :].rearrange("p a s h -> p (a s h)"),
                                 d12[:, :, :, :].rearrange("p a s h -> p (a s h)"), ACT.Exp).then_inc(rescaled, 1)

                def copy_logits(i, k, M):
                    act.wait_ge(alpha_t, M + 1)
                    if has(i, k, -1):
                        act.wait_ge(max_ready, M)
                    G.activation(aT[:, :], psT.rearrange("r (j p) -> r p j", j=J), ACT.Copy).then_inc(alpha_t_sb, 1)

                def exponentials(k, M):
                    act.wait_ge(diff_ready, M + 1)
                    ex = gbuf[:, k, :, :, 0:ROW].rearrange("p s j (h x) -> p j s h x", x=HX)[:, :, :, :, C]
                    G.activation(ex, dif[:, :, :].rearrange("p j (s h) -> p j s h", s=S), ACT.Exp
                                 ).then_inc(exp_ready, 1)

                def body(i, k):
                    M = i * SLOTS + k
                    if has(i, k, 1):
                        copy_logits(*ahead(i, k, 1), M + 1)
                        edge_onehot(*ahead(i, k, 1), M + 1)
                        exponentials((k + 1) % SLOTS, M + 1)
                    if has(i, k, 3):
                        distances(*ahead(i, k, 3), M + 3)
                    rescale(M)
                    if has(i, k, 3):
                        transposed_onehot(k)
                for k in range(2):
                    distances(0, k, k)
                    transposed_onehot(k)
                copy_logits(0, 0, 0)
                exponentials(0, 0)
                edge_onehot(0, 0, 0)
                distances(0, 2, 2)
                transposed_onehot(2)
                rounds(act, body, ch, 2 * SLOTS)

            @block.tensor
            def _(pe):
                T = nc.tensor

                def logits(i, k, M):
                    w = windows_of(mybir.EngineType.PE, M)
                    pe.wait_ge(onehot_t_ready, M + 1)
                    if has_ea:
                        pe.wait_ge(ea_in[k], i * (16 * S) + 16 * S)
                    for j in range(J):
                        if has_ea:
                            T.matmul(psA[:, j * S * H:(j + 1) * S * H], m["ea"][:, k, j:STEP:J],
                                     m["webd"][:, l, :, :].rearrange("p s h -> p (s h)"), start=True, stop=False)
                        for s in range(S):
                            c = (j * S + s) * H
                            for q in range(3):
                                last = T.matmul(
                                    psA[:, c:c + H], onehot_t[:, k, s, j:STEP:J],
                                    m["a_dst3"][:, bass.ds(w[s], 1), q, :].rearrange("p o h -> p (o h)"),
                                    start=not has_ea and q == 0, stop=q == 2 and (not has_ea or s == S - 1))
                    last.then_inc(pre_ready, 1)

                def sums(i, k, M, s):
                    pe.wait_ge(weighted, M * S + (s + 1))
                    if has(i, k, -1):
                        pe.wait_ge(merged, M * S + (s + 1 - S))
                    for j in range(J):
                        last = T.matmul(psM[:, s, 0:MSG], onehot[:, k, s * J + j, :], gbuf[:, k, s, j, :],
                                        start=j == 0, stop=j == J - 1)
                    last.then_inc(summed, 1)

                def turn_logits(i, k, M):
                    pe.wait_ge(alpha_ready, M + 1)
                    if has(i, k, -1):
                        pe.wait_ge(alpha_t_sb, M)
                    for j in range(J):
                        last = T.transpose(psT[:, j * P:(j + 1) * P], alpha[:, j, :], m["ident"][:, :])
                    last.then_inc(alpha_t, 1)

                def turn_maxima(i, k, M):
                    pe.wait_ge(max_ready, M + 1)
                    if has(i, k, -1):
                        pe.wait_ge(max_used, M)
                    pe.nop(nofuse=True)
                    for j in range(J):
                        last = T.transpose(psR[:, j * S * H:(j + 1) * S * H], mx[:, j:STEP:J],
                                           m["ident"][0:S * H, 0:S * H])
                    last.then_inc(max_back, 1)

                def body(i, k):
                    M = i * SLOTS + k
                    pe.wait_ge(onehot_ready, M + 1)
                    sums(i, k, M, 0)
                    if has(i, k, 1):
                        turn_logits(*ahead(i, k, 1), M + 1)
                    for s in range(1, S - 1):
                        sums(i, k, M, s)
                    if has(i, k, 1):
                        turn_maxima(*ahead(i, k, 1), M + 1)
                    sums(i, k, M, S - 1)
                    if has(i, k, 2):
                        logits(*ahead(i, k, 2), M + 2)
                pe.wait_ge(split_ready, 1)
                logits(0, 0, 0)
                turn_logits(0, 0, 0)
                turn_maxima(0, 0, 0)
                logits(0, 1, 1)
                rounds(pe, body)

            @block.vector
            def _(dve):
                ch = Chain(own)
                V = nc.vector

                def step_nodes(k, M):
                    ch.inc(V.tensor_copy(w4[:, k, :], m["w_base"][:, bass.ds(M * S, S)]))
                    V.tensor_scalar(nid4[:, k, :], m["w_base"][:, bass.ds(M * S, S)], m["pidx"][:, 0:1], -1.0,
                                    ALU.add, ALU.mult).then_inc(nid_ready, 1)

                def edge_nodes(i, k, M):
                    dve.wait_ge(rec_in[k], i * (16 * S) + 16 * S)
                    r = rec[:, k, :, :, :]
                    ch.inc(V.tensor_tensor(flag[:, k, :, :], r[:, :, :, 1], r[:, :, :, 2], ALU.not_equal))
                    V.tensor_tensor(dl[:, k, :, :], w4[:, k, :].unsqueeze(2).to_broadcast([P, S, J]),
                                    r[:, :, :, 1], ALU.subtract).then_inc(rec_used, 1)
                    ch.wait(dve)
                    return ch.inc(V.tensor_tensor(flag[:, k, :, :], flag[:, k, :, :], m["last_row"][:, :, :],
                                                  ALU.max))

                def merge_maxima(M, w):
                    dve.wait_ge(summed, M * S + S)
                    ch.inc(V.tensor_scalar(untouched[:, :], psM[:, :, MSG - 1], 1.0, BIG, ALU.subtract, ALU.mult))
                    ch.wait(dve)
                    ch.inc(V.tensor_tensor(part_max[:, :, :], psM[:, :, ROW:ROW + H],
                                           untouched[:, :].unsqueeze(2).to_broadcast([P, S, H]), ALU.add))
                    ch.wait(dve)
                    for s in range(S):
                        am = m["acc_max"][:, bass.ds(w[s], 1), :].rearrange("p o h -> p (o h)")
                        ch.inc(V.tensor_copy(old_max[:, s, :], am))
                        ch.wait(dve)
                        ch.inc(V.tensor_tensor(am, old_max[:, s, :], part_max[:, s, :], ALU.max))
                        ch.wait(dve)
                    ch.inc(V.tensor_tensor(new_max[:, :, :], old_max[:, :, :], part_max[:, :, :], ALU.max))
                    ch.wait(dve)
                    ch.inc(V.tensor_tensor(d12[:, 0, :, :], old_max[:, :, :], new_max[:, :, :], ALU.subtract))
                    V.tensor_tensor(d12[:, 1, :, :], part_max[:, :, :], new_max[:, :, :],
                                    ALU.subtract).then_inc(rescale_ready, 1)

                def factor(a, s):
                    return r12[:, a, s, :].unsqueeze(2).to_broadcast([P, H, HX])

                def scale_parts(M):
                    dve.wait_ge(rescaled, M + 1)
                    for s in range(S):
                        V.tensor_tensor(part[:, s, :, :], psM[:, s, 0:ROW].rearrange("p (h x) -> p h x", x=HX),
                                        factor(1, s), ALU.mult).then_inc(merged, 1)

                def accumulate(M, w):
                    dve.wait_ge(merged, M * S + S)
                    for s in range(S):
                        acc = m["acc"][:, bass.ds(w[s], 1), :, :].rearrange("p o h x -> p (o h) x")
                        ch.wait(dve)
                        ch.inc(V.tensor_tensor(acc, acc, factor(0, s), ALU.mult))
                        yield
                        ch.wait(dve)
                        ch.inc(V.tensor_tensor(acc, acc, part[:, s, :, :], ALU.add))
                        yield

                def add_sources(i, k, M):
                    dve.wait_ge(pre_ready, M + 1)
                    dve.wait_ge(gathered[k], i * (16 * S * J) + 16 * S * J)
                    a_src = gbuf[:, k, :, :, 0:ROW].rearrange("p s j (h x) -> p j s h x", x=HX)[:, :, :, :, C]
                    ch.inc(V.tensor_tensor(asum[:, :, :].rearrange("p j (s h) -> p j s h", s=S),
                                           psA.rearrange("p (j s h) -> p j s h", j=J, s=S), a_src, ALU.add))
                    ch.wait(dve)
                    V.scalar_tensor_tensor(alpha[:, :, :], asum[:, :, :], 0.2, asum[:, :, :], ALU.mult,
                                           ALU.max).then_inc(alpha_ready, 1)

                def segment_maxima(i, k, M):
                    dve.wait_ge(link_in[k], i * (16 * S) + 16 * S)
                    dve.wait_ge(alpha_t_sb, M + 1)
                    ch.inc(V.tensor_tensor_scan(fwd[:, :], link[:, k, 0:STEP], aT[:, :], -BIG, ALU.add, ALU.max))
                    ch.wait(dve)
                    V.tensor_tensor_scan(mx[:, ::-1], link[:, k, :0:-1], fwd[:, ::-1], -BIG,
                                         ALU.add, ALU.max).then_inc(max_ready, 1)

                def differences(k, M):
                    dve.wait_ge(alpha_ready, M + 1)
                    dve.wait_ge(max_back, M + 1)
                    V.tensor_tensor(dif[:, :, :], alpha[:, :, :], psR.rearrange("p (j c) -> p j c", j=J),
                                    ALU.subtract).then_inc(diff_ready, 1)
                    V.tensor_tensor(gbuf[:, k, :, :, ROW:ROW + H].rearrange("p s j h -> p j s h"),
                                    psR.rearrange("p (j s h) -> p j s h", j=J, s=S),
                                    flag[:, k, :, :].rearrange("p s j -> p j s").unsqueeze(3)
                                    .to_broadcast([P, J, S, H]), ALU.mult).then_inc(max_used, 1)
                    ch.inc(V.tensor_copy(gbuf[:, k, :, :, MSG - 1], flag[:, k, :, :]))

                def weigh(k, s):
                    g = gbuf[:, k, s, :, 0:ROW].rearrange("p j (h x) -> p j h x", x=HX)
                    V.tensor_tensor(g[:, :, :, 0:C], g[:, :, :, 0:C],
                                    g[:, :, :, C:HX].to_broadcast([P, J, H, C]), ALU.mult).then_inc(weighted, 1)

                def body(i, k):
                    M = i * SLOTS + k
                    dve.wait_ge(exp_ready, M + 1)
                    weigh(k, 0)
                    if has(i, k, -1):
                        scale_parts(M - 1)
                        w = windows_of(mybir.EngineType.DVE, M - 1, 2)
                        steps = accumulate(M - 1, w[:S])
                    else:
                        w = windows_of(mybir.EngineType.DVE, M)
                        steps = iter(())
                    if has(i, k, 1):
                        add_sources(*ahead(i, k, 1), M + 1)
                    for s in range(1, S):
                        weigh(k, s)
                        next(steps, None)
                    if has(i, k, 1):
                        segment_maxima(*ahead(i, k, 1), M + 1)
                    for _ in steps:
                        pass
                    if has(i, k, 2):
                        edge_nodes(*ahead(i, k, 2), M + 2)
                    if has(i, k, 3):
                        step_nodes(k, M + 3)
                    if has(i, k, 1):
                        differences((k + 1) % SLOTS, M + 1)
                    ch.wait(dve)
                    merge_maxima(M, w[-S:])

                a, a3 = m["a_dst"][:, :, :], m["a_dst3"]
                for q in range(3):
                    ch.inc(V.tensor_copy(a3[:, :, q, :], a))
                    ch.wait(dve)
                    if q < 2:
                        ch.inc(V.tensor_tensor(a, a, a3[:, :, q, :], ALU.subtract))
                        ch.wait(dve)
                dve.sem_inc(split_ready, 1)
                for k in range(SLOTS):
                    step_nodes(k, k)
                ch.wait(dve)
                edge_nodes(0, 0, 0)
                edge_nodes(0, 1, 1)
                ch.wait(dve)
                add_sources(0, 0, 0)
                segment_maxima(0, 0, 0)
                differences(0, 0)
                rounds(dve, body, ch, SLOTS * (2 * S + 1 + 1 + 2 + 1 + 1 + (2 + 2 * S + 2)))
                M = MACROS - 1
                w = windows_of(mybir.EngineType.DVE, M)
                scale_parts(M)
                for _ in accumulate(M, w):
                    pass


def nodes_out(nc, sem, A, m, psum, x1_dram, res_dram, out):
    v = scratch(m, {"res": (2, F), "x1": (2, F), "o": (2, F), "o_t": (KT, 2 * P), "den": (2, H),
                    "stat": (2, 6), "mv": (2, 2), "rstd": (2, 1), "stat2": (2, 6), "mv2": (2, 2), "rstd2": (2, 1),
                    "skip": (2, F), "y": (2, F), "eps": (1,), "w1": (KT, FF), "w2": (FT, F), "g": (FT, 2 * P)})
    (w_in, own, res_in, x1_in, stored, res_used, x1_used, o_ready, o_tr, o_t_ready, up, gelu, down, down_used, var,
     std, var2, std2, out_ready) = (
        sem(k + "_o") for k in ("ffn_in", "dve", "res_in", "x1_in", "stored", "res_used", "x1_used", "o_ready",
                                "o_tr", "o_t_ready", "up", "gelu", "down", "down_used", "var", "std", "var2", "std2",
                                "out_ready"))

    with nc.Block() as block:
        @block.sync
        def _(sp):
            sp.dma_start(v["res"], load_pair(res_dram, 0)).then_inc(res_in, 16)
            sp.dma_start(v["w1"], A["L1_gnn_ffn_w1"].rearrange("(k p) c -> p k c", p=P)).then_inc(w_in, 16)
            sp.dma_start(v["w2"], A["L1_gnn_ffn_w2"].rearrange("(k p) c -> p k c", p=P)).then_inc(w_in, 16)

            def body(i):
                if is_later(i):
                    sp.wait_ge(x1_used, i)
                    sp.nop(nofuse=True)
                sp.dma_start(v["x1"], load_pair(x1_dram, i)).then_inc(x1_in, 16)
                if has_next(i):
                    sp.wait_ge(res_used, i + 1)
                    sp.nop(nofuse=True)
                    sp.dma_start(v["res"], load_pair(res_dram, i + 1)).then_inc(res_in, 16)
            pairs(sp, body)

        @block.gpsimd
        def _(pool):
            def body(i):
                pool.wait_ge(out_ready, i + 1)
                pool.nop(nofuse=True)
                pool.dma_start(load_pair(out, i), v["y"]).then_inc(stored, 16)
            pairs(pool, body)
            pool.wait_ge(stored, 16 * PAIRS)

        @block.scalar
        def _(act):
            def deviations(i, ready, mv, rs, done):
                act.wait_ge(ready, i + 1)
                nc.scalar.activation(v[rs], v[mv][:, :, 1:2], ACT.Sqrt, bias=v["eps"][:, 0:1]).then_inc(done, 1)

            def transposed(i):
                act.wait_ge(o_tr, i + 1)
                nc.scalar.activation(v["o_t"], psum[:, 0, :].rearrange("p (k n) -> p k n", k=KT),
                                     ACT.Copy).then_inc(o_t_ready, 1)

            def body(i):
                for f in range(FT):
                    act.wait_ge(up, i * FT + (f + 1))
                    if f == 0 and is_later(i):
                        act.wait_ge(down, i * 2)
                    nc.scalar.activation(v["g"][:, f, :], psum[:, 1 + f % 3, 0:2 * P], ACT.Gelu_apprx_tanh,
                                         bias=m["fb1"][:, f:f + 1]).then_inc(gelu, 1)
                if is_later(i):
                    deviations(i - 1, var2, "mv2", "rstd2", std2)
                if has_next(i):
                    deviations(i + 1, var, "mv", "rstd", std)
                    transposed(i + 1)
            act.wait_ge(own, 1)
            deviations(0, var, "mv", "rstd", std)
            transposed(0)
            pairs(act, body)
            deviations(PAIRS - 1, var2, "mv2", "rstd2", std2)

        @block.tensor
        def _(pe):
            T = nc.tensor

            def transposes(i):
                pe.wait_ge(o_ready, i + 1)
                if is_later(i):
                    pe.wait_ge(o_t_ready, i)
                for b in range(2):
                    for k in range(KT):
                        last = T.transpose(psum[:, 0, (2 * k + b) * P:(2 * k + b + 1) * P],
                                           v["o"][:, b, k * P:(k + 1) * P], m["ident"][:, :])
                last.then_inc(o_tr, 1)

            def body(i):
                pe.wait_ge(o_t_ready, i + 1)
                for f in range(FT):
                    if f >= 3:
                        pe.wait_ge(gelu, i * FT + (f - 2))
                    for k in range(KT):
                        last = T.matmul(psum[:, 1 + f % 3, 0:2 * P], v["w1"][:, k, f * P:(f + 1) * P],
                                        v["o_t"][:, k, :], start=k == 0, stop=k == KT - 1)
                    last.then_inc(up, 1)
                for b in range(2):
                    if b == 0 and is_later(i):
                        pe.wait_ge(down_used, i)
                    for f in range(FT):
                        if b == 0:
                            pe.wait_ge(gelu, i * FT + (f + 1))
                        if b == 1 and f == FT - 3 and has_next(i):
                            transposes(i + 1)
                        last = T.matmul(psum[:, 4 + b, 0:F], v["g"][:, f, b * P:(b + 1) * P], v["w2"][:, f, :],
                                        start=f == 0, stop=f == FT - 1)
                    last.then_inc(down, 1)
            transposes(0)
            pe.wait_ge(w_in, 32)
            pairs(pe, body)

        @block.vector
        def _(dve):
            ch = Chain(own)
            V = nc.vector

            def on_both(row):
                return m["vec"][:, row, :].unsqueeze(1).to_broadcast([P, 2, F])

            def stats(src, stat, mv, done):
                for b in range(2):
                    ch.inc(V.bn_stats(v[stat][:, b, :], src[:, b, :]))
                ch.wait(dve)
                dve.nop(nofuse=True)
                V.bn_aggr(v[mv][:, 0, :], v[stat][:, 0, :])
                V.bn_aggr(v[mv][:, 1, :], v[stat][:, 1, :]).then_inc(done, 1)

            def attention(i):
                acc = m["acc"][:, bass.ds(i * 2, 2), :, :].rearrange("p b h x -> p (b h) x")
                den, o = v["den"].rearrange("p b h -> p (b h)"), v["o"]
                ch.inc(V.reciprocal(den, acc[:, :, C:HX].rearrange("p h o -> p (h o)")))
                ch.wait(dve)
                if is_later(i):
                    dve.wait_ge(o_tr, i)
                ch.inc(V.tensor_tensor(o.rearrange("p b (h c) -> p (b h) c", c=C), acc[:, :, 0:C],
                                       den.unsqueeze(2).to_broadcast([P, 2 * H, C]), ALU.mult))
                ch.wait(dve)
                dve.wait_ge(res_in, i * 16 + 16)
                V.tensor_tensor(o, o, v["res"], ALU.add).then_inc(res_used, 1)
                dve.wait_ge(res_used, i + 1)
                stats(o, "stat", "mv", var)

            def norm(i):
                o = v["o"]
                dve.wait_ge(std, i + 1)
                ch.inc(V.reciprocal(v["rstd"], v["rstd"]))
                ch.wait(dve)
                for b in range(2):
                    ch.inc(V.tensor_scalar(o[:, b, :], o[:, b, :], v["mv"][:, b, 0:1], v["rstd"][:, b, 0:1],
                                           ALU.subtract, ALU.mult))
                ch.wait(dve)
                ch.inc(V.tensor_tensor(o, o, on_both(VG2), ALU.mult))
                ch.wait(dve)
                V.tensor_tensor(o, o, on_both(VE2), ALU.add).then_inc(o_ready, 1)

            def skips(i):
                dve.wait_ge(o_ready, i + 1)
                dve.wait_ge(x1_in, i * 16 + 16)
                V.tensor_tensor(v["skip"], v["o"], v["x1"], ALU.add).then_inc(x1_used, 1)
                dve.wait_ge(x1_used, i + 1)
                ch.inc(V.tensor_tensor(v["skip"], v["skip"], on_both(VFB2), ALU.add))
                ch.wait(dve)

            def ffn_sum(i):
                dve.wait_ge(down, i * 2 + 2)
                if is_later(i):
                    dve.wait_ge(stored, i * 16)
                V.tensor_tensor(v["y"], v["skip"], psum[:, 4:6, 0:F], ALU.add).then_inc(down_used, 1)
                dve.wait_ge(down_used, i + 1)
                stats(v["y"], "stat2", "mv2", var2)

            def last_norm(i):
                dve.wait_ge(std2, i + 1)
                ch.inc(V.reciprocal(v["rstd2"], v["rstd2"]))
                ch.wait(dve)
                for b in range(2):
                    last = V.tensor_scalar(v["y"][:, b, :], v["y"][:, b, :], v["mv2"][:, b, 0:1],
                                           v["rstd2"][:, b, 0:1], ALU.subtract, ALU.mult)
                last.then_inc(out_ready, 1)

            def body(i):
                if is_later(i):
                    ffn_sum(i - 1)
                skips(i)
                if has_next(i):
                    attention(i + 1)
                if is_later(i):
                    last_norm(i - 1)
                if has_next(i):
                    norm(i + 1)

            ch.inc(V.memset(v["eps"], 1e-5))
            ch.wait(dve)
            attention(0)
            norm(0)
            body(0)
            per = 2 + 1 + (1 + 1 + 2) + 1 + (1 + 2 + 1)
            with dve.Fori(1, PAIRS - 1) as i:
                ch.enter(i, 1, per)
                body(i)
                ch.leave(PAIRS - 1)
            body(PAIRS - 1)
            ffn_sum(PAIRS - 1)
            last_norm(PAIRS - 1)


def kernel(**inputs):
    import concourse.bacc as bacc
    from concourse.bass_utils import run_bass_kernel_spmd

    a = {k: np.ascontiguousarray(v) for k, v in inputs.items()}
    x = np.pad(a["x"], ((0, NP - N), (0, 0)))
    src = np.pad(a["src"], (0, EP - E))
    dst = np.pad(a["dst"], (0, EP - E), constant_values=NO_NODE)
    arrays = {
        "x": x, "dst": dst,
        "records": np.ascontiguousarray(np.stack([src, dst, np.roll(dst, -1), np.zeros_like(dst)], axis=1)),
        "ea_t": np.ascontiguousarray(np.pad(a["edge_attr_16"], ((0, EP - E), (0, 0))).T),
        "ffn_b1_cols": np.ascontiguousarray(a["L1_gnn_ffn_b1"].reshape(FT, P).T),
    }
    for k in a:
        if k not in ("x", "src", "dst", "edge_attr_16", "L1_gnn_ffn_b1"):
            arrays[k] = a[k]
    nc = bacc.Bacc("TRN2", target_bir_lowering=False, num_devices=1)
    A = {k: nc.dram_tensor(f"in_{k}", v.shape, mybir.dt.from_np(v.dtype), kind="ExternalInput").ap()
         for k, v in arrays.items()}
    out = nc.dram_tensor("out_0", [NP, F], F32, kind="ExternalOutput").ap()
    build(nc, A, out)
    r = run_bass_kernel_spmd(nc, [{f"in_{k}": v for k, v in arrays.items()}], core_ids=[0])
    return np.ascontiguousarray(r.results[0]["out_0"][:N])
```
